# Optimizing a Trainium2 kernel written in Bass

```python
import numpy as np
import jax
import jax.numpy as jnp

def _softmax(x, axis=-1):
    return jax.nn.softmax(x, axis=axis)

def _gelu(x):
    return jax.nn.gelu(x, approximate=True)

def _silu(x):
    return jax.nn.silu(x)

def _sigmoid(x):
    return jax.nn.sigmoid(x)

def _layernorm(x, axis=-1, eps=1e-05):
    m = jnp.mean(x, axis=axis, keepdims=True)
    v = jnp.var(x, axis=axis, keepdims=True)
    return (x - m) / jnp.sqrt(v + eps)

def _scatter_add(tgt, idx, src, axis=0):
    return tgt.at[idx].add(src)

def _segment_sum(src, seg, n):
    return jax.ops.segment_sum(src, seg, n)
kernel_name = 'mk_vit_tower_d1_tok_img768_r4_5b71d8'

def setup_inputs(seed: int=0):
    np.random.seed(seed)
    _w = jnp.asarray

    def _rec_inputs():
        import jax
        import jax.numpy as jnp
        _rk = jax.random.key(seed)
        x = -0.00016672 + 0.999947 * jax.random.normal(jax.random.fold_in(_rk, 1), (64, 3, 224, 224), jnp.float32)
        return x
    x = _rec_inputs()

    def _L0_tok_setup():
        import jax, jax.numpy as jnp
        import numpy as np
        EPS = 1e-05

        def _layernorm(x, g, b):
            m = jnp.mean(x, axis=-1, keepdims=True)
            v = jnp.mean(jnp.square(x - m), axis=-1, keepdims=True)
            return (x - m) * jax.lax.rsqrt(v + EPS) * g + b
        key = jax.random.key(seed)
        ks = jax.random.split(key, 4)
        B, C, H, Wd, P, D = (64, 3, 96, 96, 16, 192)
        pd = P * P * C
        return {'x': jax.random.normal(ks[0], (B, C, H, Wd), dtype=jnp.float32), 'ln1_g': jnp.ones((pd,), jnp.float32), 'ln1_b': jnp.zeros((pd,), jnp.float32), 'W': jax.random.normal(ks[1], (pd, D), dtype=jnp.float32) * pd ** (-0.5), 'b': jnp.zeros((D,), jnp.float32), 'ln2_g': jnp.ones((D,), jnp.float32), 'ln2_b': jnp.zeros((D,), jnp.float32), 'cls': jax.random.normal(ks[2], (1, 1, D), dtype=jnp.float32)}
    _L0_tok_all = _L0_tok_setup()
    _L0_tok_in = {k: v for k, v in _L0_tok_all.items() if k in ('ln1_g', 'ln1_b', 'W', 'b', 'ln2_g', 'ln2_b', 'cls')}
    del _L0_tok_all

    def _L0_attn_setup():
        import jax, jax.numpy as jnp
        import numpy as np
        DIM = 192
        HEADS = 12
        DIM_HEAD = 64
        INNER = HEADS * DIM_HEAD
        L = 64
        EPS = 1e-08
        key = jax.random.key(seed)
        k1, k2, k3, k4 = jax.random.split(key, 4)
        x = jax.random.normal(k1, (2, 1024, DIM), dtype=jnp.float32)
        w_qkv = jax.random.normal(k2, (3 * INNER, DIM), dtype=jnp.float32) * DIM ** (-0.5)
        w_out = jax.random.normal(k3, (DIM, INNER), dtype=jnp.float32) * INNER ** (-0.5)
        b_out = jax.random.normal(k4, (DIM,), dtype=jnp.float32) * 0.01
        scale = jnp.full((HEADS,), np.log2(L * L - L), dtype=jnp.float32)
        return {'x': x, 'w_qkv': w_qkv, 'w_out': w_out, 'b_out': b_out, 'scale': scale}
    _L0_attn_all = _L0_attn_setup()
    _L0_attn_in = {k: v for k, v in _L0_attn_all.items() if k in ('w_qkv', 'w_out', 'b_out', 'scale')}
    del _L0_attn_all

    def _L0_ffn_setup():
        import jax, jax.numpy as jnp
        import numpy as np
        DIM = 192
        NUM_HEADS = 12
        HEAD_DIM = DIM // NUM_HEADS
        SCALE = HEAD_DIM ** (-0.5)
        NUM_EXPERTS = 8
        RANK = 16
        ALPHA = 32
        TOPK = 2
        SCALING = ALPHA / RANK
        B, S = (8, 256)
        key = jax.random.key(seed)
        ks = jax.random.split(key, 12)
        d, e, r = (DIM, NUM_EXPERTS, RANK)
        inp = {'x': jax.random.normal(ks[0], (B, S, d), jnp.float32), 'Wg': jax.random.normal(ks[1], (e, d), jnp.float32) * 0.02, 'bg': jax.random.normal(ks[2], (e,), jnp.float32) * 0.02, 'Wqkv': jax.random.normal(ks[3], (3 * d, d), jnp.float32) * 0.02, 'bqkv': jax.random.normal(ks[4], (3 * d,), jnp.float32) * 0.02, 'Wproj': jax.random.normal(ks[5], (d, d), jnp.float32) * 0.02, 'bproj': jax.random.normal(ks[6], (d,), jnp.float32) * 0.02, 'A': jax.random.normal(ks[7], (e, r, d), jnp.float32) * 0.05, 'ba': jax.random.normal(ks[8], (e, r), jnp.float32) * 0.02, 'Bm': jax.random.normal(ks[9], (e, 3 * d, r), jnp.float32) * 0.05, 'bb': jax.random.normal(ks[10], (e, 3 * d), jnp.float32) * 0.02}
        return inp
    _L0_ffn_all = _L0_ffn_setup()
    _L0_ffn_in = {k: v for k, v in _L0_ffn_all.items() if k in ('Wg', 'bg', 'Wqkv', 'bqkv', 'Wproj', 'bproj', 'A', 'ba', 'Bm', 'bb')}
    del _L0_ffn_all
    return {'x': x, 'L0_tok_ln1_g': _L0_tok_in['ln1_g'], 'L0_tok_ln1_b': _L0_tok_in['ln1_b'], 'L0_tok_W': _L0_tok_in['W'], 'L0_tok_b': _L0_tok_in['b'], 'L0_tok_ln2_g': _L0_tok_in['ln2_g'], 'L0_tok_ln2_b': _L0_tok_in['ln2_b'], 'L0_tok_cls': _L0_tok_in['cls'], 'L0_attn_w_qkv': _L0_attn_in['w_qkv'], 'L0_attn_w_out': _L0_attn_in['w_out'], 'L0_attn_b_out': _L0_attn_in['b_out'], 'L0_attn_scale': _L0_attn_in['scale'], 'L0_ffn_Wg': _L0_ffn_in['Wg'], 'L0_ffn_bg': _L0_ffn_in['bg'], 'L0_ffn_Wqkv': _L0_ffn_in['Wqkv'], 'L0_ffn_bqkv': _L0_ffn_in['bqkv'], 'L0_ffn_Wproj': _L0_ffn_in['Wproj'], 'L0_ffn_bproj': _L0_ffn_in['bproj'], 'L0_ffn_A': _L0_ffn_in['A'], 'L0_ffn_ba': _L0_ffn_in['ba'], 'L0_ffn_Bm': _L0_ffn_in['Bm'], 'L0_ffn_bb': _L0_ffn_in['bb']}

def reference(x, L0_tok_ln1_g, L0_tok_ln1_b, L0_tok_W, L0_tok_b, L0_tok_ln2_g, L0_tok_ln2_b, L0_tok_cls, L0_attn_w_qkv, L0_attn_w_out, L0_attn_b_out, L0_attn_scale, L0_ffn_Wg, L0_ffn_bg, L0_ffn_Wqkv, L0_ffn_bqkv, L0_ffn_Wproj, L0_ffn_bproj, L0_ffn_A, L0_ffn_ba, L0_ffn_Bm, L0_ffn_bb):
    import jax
    import jax.numpy as jnp

    def _L0_tok_ref(x, ln1_g, ln1_b, W, b, ln2_g, ln2_b, cls):
        import jax, jax.numpy as jnp
        import numpy as np
        EPS = 1e-05

        def _layernorm(x, g, b):
            m = jnp.mean(x, axis=-1, keepdims=True)
            v = jnp.mean(jnp.square(x - m), axis=-1, keepdims=True)
            return (x - m) * jax.lax.rsqrt(v + EPS) * g + b
        P = 16
        B, C, H, Wd = x.shape
        Hp, Wp = (H // P, Wd // P)
        p = x.reshape(B, C, Hp, P, Wp, P).transpose(0, 2, 4, 3, 5, 1).reshape(B, Hp * Wp, P * P * C)
        h = _layernorm(p, ln1_g, ln1_b)
        h = jnp.einsum('bnd,de->bne', h, W) + b
        h = _layernorm(h, ln2_g, ln2_b)
        cls_toks = jnp.broadcast_to(cls, (B, 1, cls.shape[-1]))
        return jnp.concatenate([cls_toks, h], axis=1)

    def _L0_attn_ref(x, w_qkv, w_out, b_out, scale):
        import jax, jax.numpy as jnp
        import numpy as np
        DIM = 192
        HEADS = 12
        DIM_HEAD = 64
        INNER = HEADS * DIM_HEAD
        L = 64
        EPS = 1e-08
        b, n, d = x.shape
        h, dh = (HEADS, DIM_HEAD)
        qkv = x @ w_qkv.T
        q, k, v = jnp.split(qkv, 3, axis=-1)
        q, k, v = (t.reshape(b, n, h, dh).transpose(0, 2, 1, 3) for t in (q, k, v))
        q = q * jax.lax.rsqrt(jnp.linalg.norm(q, axis=1, keepdims=True) + EPS)
        k = k * jax.lax.rsqrt(jnp.linalg.norm(k, axis=1, keepdims=True) + EPS)
        dots = jnp.einsum('bhid,bhjd->bhij', q, k)
        scores = jax.nn.softmax(dots / scale[:, None, None], axis=-1)
        out = jnp.einsum('bhij,bhjd->bhid', scores, v)
        out = out.transpose(0, 2, 1, 3).reshape(b, n, h * dh)
        return out @ w_out.T + b_out

    def _L0_ffn_ref(x, Wg, bg, Wqkv, bqkv, Wproj, bproj, A, ba, Bm, bb):
        import jax, jax.numpy as jnp
        import numpy as np
        DIM = 192
        NUM_HEADS = 12
        HEAD_DIM = DIM // NUM_HEADS
        SCALE = HEAD_DIM ** (-0.5)
        NUM_EXPERTS = 8
        RANK = 16
        ALPHA = 32
        TOPK = 2
        SCALING = ALPHA / RANK
        B, S = (8, 256)
        b, s, d = x.shape
        t = b * s
        xf = x.reshape(t, d)
        probs = jax.nn.softmax(xf @ Wg.T + bg, axis=-1)
        top_w, top_idx = jax.lax.top_k(probs, TOPK)
        combine = jnp.zeros((t, NUM_EXPERTS), x.dtype).at[jnp.arange(t)[:, None], top_idx].add(top_w)
        h = jnp.einsum('td,erd->ter', xf, A) + ba
        hw = h * combine[:, :, None]
        delta = jnp.einsum('ter,eor->to', hw, Bm) + combine @ bb
        delta = delta * SCALING
        qkv = xf @ Wqkv.T + bqkv + delta
        qkv = qkv.reshape(b, s, 3, NUM_HEADS, HEAD_DIM)
        qkv = jnp.transpose(qkv, (2, 0, 3, 1, 4))
        q, k, v = (qkv[0], qkv[1], qkv[2])
        attn = jax.nn.softmax(jnp.einsum('bhsd,bhtd->bhst', q, k) * SCALE, axis=-1)
        out = jnp.einsum('bhst,bhtd->bhsd', attn, v)
        out = jnp.transpose(out, (0, 2, 1, 3)).reshape(b, s, d)
        return out @ Wproj.T + bproj
    h = _L0_tok_ref(x, L0_tok_ln1_g, L0_tok_ln1_b, L0_tok_W, L0_tok_b, L0_tok_ln2_g, L0_tok_ln2_b, L0_tok_cls)
    h = h + _L0_attn_ref(_layernorm(h, axis=-1), L0_attn_w_qkv, L0_attn_w_out, L0_attn_b_out, L0_attn_scale)
    h = h + _L0_ffn_ref(_layernorm(h, axis=-1), L0_ffn_Wg, L0_ffn_bg, L0_ffn_Wqkv, L0_ffn_bqkv, L0_ffn_Wproj, L0_ffn_bproj, L0_ffn_A, L0_ffn_ba, L0_ffn_Bm, L0_ffn_bb)
    return h

_drawn_inputs = setup_inputs


def setup_inputs(seed=0):
    import zlib

    import numpy as np

    out = dict(_drawn_inputs(seed))
    spreads = {'L0_tok_ln1_g': (1.0, 0.2),
     'L0_tok_ln1_b': (0.0, 0.1),
     'L0_tok_b': (0.0, 0.1),
     'L0_tok_ln2_g': (1.0, 0.2),
     'L0_tok_ln2_b': (0.0, 0.1),
     'L0_attn_scale': (11.977279663085938, 0.6)}
    factors = {'L0_attn_b_out': 6.227,
     'L0_ffn_Wg': 8.0,
     'L0_ffn_bg': 8.0,
     'L0_ffn_Wqkv': 3.29,
     'L0_ffn_bqkv': 8.0,
     'L0_ffn_Wproj': 3.073,
     'L0_ffn_bproj': 22.784,
     'L0_ffn_A': 8.0,
     'L0_ffn_ba': 8.0,
     'L0_ffn_Bm': 8.0,
     'L0_ffn_bb': 8.0}
    for name, (base, spread) in spreads.items():
        noise = np.random.default_rng([zlib.crc32(name.encode()), seed]).standard_normal(out[name].shape)
        drawn = base * np.exp(spread * noise) if base else spread * noise
        out[name] = jnp.asarray(drawn.astype(out[name].dtype))
    for name, factor in factors.items():
        out[name] = (out[name] * factor).astype(out[name].dtype)
    return out
```

```python
import numpy as np
import concourse.bass as bass
from concourse import mybir
from contextlib import ExitStack

B, D, NP = 64, 192, 196
NT = NP + 1
PD, KC = 768, 6
TR, TO = 99, 98
H, DH = 12, 64
DH2 = D // H
INNER = H * DH
NE, RANK = 8, 16
HC = D // 2
ITERS = B // 2
EPS = 1e-5
LORA_SCALE = 32 / RANK
QSCALE = DH2 ** -0.5

SCHED = []
for kind, count in (("EMB", 1), ("T1", 1), ("QK", 3), ("PS", 1), ("V", 2), ("SM", 6), ("NT", 1),
                    ("ATT", 6), ("OP", 1), ("T2", 1), ("G", 1), ("T3", 1), ("QK2", 1), ("V2", 1),
                    ("SM2", 6), ("NT2", 1), ("ATT2", 6), ("OP2", 1)):
    for s in range(2):
        for i in range(count):
            if kind == "ATT":
                SCHED.append(("ST", s, i))
                if i >= 1:
                    SCHED.append(("PV", s, i - 1))
            elif kind == "ATT2":
                SCHED.append(("ST2", s, i))
                if i in (2, 4):
                    SCHED.append(("PV2", s, i // 2 - 1))
            else:
                SCHED.append((kind, s, i))
        if kind == "ATT":
            SCHED.append(("PV", s, 5))
        if kind == "ATT2":
            SCHED.append(("PV2", s, 2))
WIDE = ("QK", "V", "SM", "ST", "QK2", "SM2", "ST2")
EBUFS = 3


def place():
    bank, before, last, wide, narrow = {}, {}, {}, 0, 0
    for p in SCHED:
        if p[0] in WIDE:
            b, wide = 2 * (wide % 3), wide + 1
        else:
            b, narrow = 6 + narrow % 2, narrow + 1
        bank[p], before[p], last[b] = b, last.get(b), p
    return bank, before, last


def vit_tower(nc, x_t, w_emb, ln1, ln1_bias, tok_const, w_qk, w_v, w_out, w_gl, w_qkv2, w_lora_b,
              w_bias2, w_proj, scale, row_const, mats, sel, out):
    F32, BF16 = mybir.dt.float32, mybir.dt.bfloat16
    ALU, ACT, AX = mybir.AluOpType, mybir.ActivationFunctionType, mybir.AxisListType
    ctx = ExitStack()
    with ctx:
        def sb(name, shape, dt=F32):
            return ctx.enter_context(nc.sbuf_tensor(name, shape, dt))

        def two(name, shape, dt=F32):
            return [sb(f"{name}{s}", shape, dt) for s in range(2)]

        def sem(name):
            return ctx.enter_context(nc.semaphore(name))

        emb_w = sb("emb_w", [128, KC, D + 1])
        ln1_sb = sb("ln1_sb", [128, KC])
        tokc = sb("tokc", [TR, 3, 2, D])
        emb_cs = sb("emb_cs", [TR, D])
        emb_b = sb("emb_b", [TR, D])
        qk_w = sb("qk_w", [HC, 2, 2 * INNER])
        v_w = sb("v_w", [HC, 2, INNER])
        out_w = sb("out_w", [128, H // 2, D])
        gl_w = sb("gl_w", [HC, 2, NE + NE * RANK])
        qkv2_w = sb("qkv2_w", [HC, 2, 3 * D])
        lorab_w = sb("lorab_w", [128, 3 * D])
        bias2_w = sb("bias2_w", [NE + 1, 3 * D])
        proj_w = sb("proj_w", [128, 3, D])
        scale_sb = sb("scale_sb", [128, H // 2])
        inv_scale = sb("inv_scale", [128, H // 2])
        rowc = sb("rowc", [TR, 2 * D + NE + NE * RANK])
        mats_sb = sb("mats_sb", [128, 258])
        ident, pair_sum = mats_sb[:, 0:128], mats_sb[:, 128:256]
        parity = [mats_sb[:, 256:257], mats_sb[:, 257:258]]
        sel_b = sb("sel_b", [128, 2, H, TR], BF16)
        ones = sb("ones", [128, TR])
        b_out, b_proj = rowc[:, 0:D], rowc[:, D:2 * D]
        b_gl = rowc[:, 2 * D:]

        xb = two("xb", [128, KC, NT])
        xss = two("xss", [128, NT])
        h0, h1 = two("h0", [TR, 2, D]), two("h1", [TR, 2, D])
        hn = two("hn", [TR, 2, D])
        hn_t, hn2_t = two("hn_t", [HC, 2, NT]), two("hn2_t", [HC, 2, NT])
        qk = two("qk", [128, H, NT])
        qk_sq = sb("qk_sq", [128, H, NT])
        xsq = qk_sq[:, 0:KC, :]
        qk_b = two("qk_b", [128, H, NT], BF16)
        emb_raw = qk_sq[:].rearrange("p m t -> p (m t)")[:, 0:KC * D].rearrange("p (c d) -> p c d", c=KC)
        ln1b_sb = qk[1][:].rearrange("p m t -> p (m t)")[:, 0:KC * TR].rearrange("p (c t) -> p c t", c=KC)
        sel_f = qk[0][:].rearrange("p m t -> p (m t)")[:, 0:2 * H].rearrange("p (a h) -> p a h", a=2)
        ss = two("ss", [128, 2, NT])
        nrm = two("nrm", [128, 2 * NT])
        vx = two("vx", [TR, 2, H, 2 * DH])
        mx = two("mx", [TR, 2, H])
        neg = two("neg", [TR, 2, 4, 32])
        neg_t = two("neg_t", [128, NT], BF16)
        ebuf = [sb(f"ebuf{i}", [TR, 2, 2, NT]) for i in range(EBUFS)]
        rinv = two("rinv", [DH, 2 * NT])
        half_neg, eps_ln = sb("half_neg", [TR, 2]), sb("eps_ln", [TR, 2])
        tiny, eps_qk = sb("tiny", [128, 1]), sb("eps_qk", [128, 1])
        o_t = two("o_t", [128, H // 2, NT])
        gl = two("gl", [TR, 2, NE + NE * RANK])
        gmax = sb("gmax", [TR, 2])
        gates = two("gates", [TR, 2, 16])
        top8 = sb("top8", [TR, 2, 8])
        rest = sb("rest", [TR, 2, 16])
        gsum = sb("gsum", [TR, 2])
        comb = two("comb", [TR, 2, NE + 1])
        hw = two("hw", [TR, 2, NE, RANK])
        hw_t, comb_t = two("hw_t", [128, NT]), two("comb_t", [NE + 1, NT])
        q2, q2b = two("q2", [128, 2, NT]), two("q2b", [128, 2, NT], BF16)
        k2, k2b = two("k2", [128, 2, 2, NT]), two("k2b", [128, 2, 2, NT], BF16)
        v2 = two("v2", [TR, 2, H, 2 * DH2])
        sums2 = two("sums2", [128, NT])
        o2_t = two("o2_t", [128, 3, NT])
        res = h1
        st6 = sb("st6", [TR, 2, 6])
        mv = sb("mv", [TR, 2, 2])
        rstd = sb("rstd", [TR, 2])
        veps = sb("veps", [TR, 2])
        lnt = sb("lnt", [TR, 2, D])
        nmean = sb("nmean", [TR, 2])
        msq = sb("msq", [TR, 2])

        psum = ctx.enter_context(nc.psum_tensor("psum", [128, 8, 512], F32))
        bank, before, last = place()

        steps = {}

        def signal(name, kinds):
            steps[name] = [p for p in SCHED if p[0] in kinds]
            return name, sem(name)

        pe_sig = {k: signal("made_" + k, (k,)) for k in
                  ("EMB", "T1", "QK", "PS", "V", "SM", "NT", "ST", "PV", "OP", "T2", "G", "T3",
                   "QK2", "V2", "SM2", "NT2", "ST2", "PV2", "OP2")}
        rd_sig = {k: signal("read_" + k, (k,)) for k in pe_sig}
        hn_ready = signal("hn_ready", ("EMB",))
        xss_ready = signal("xss_ready", ("EMB",))
        xsq_ready = signal("xsq_ready", ("EMB",))
        ss_ready = signal("ss_ready", ("PS",))
        qkn_ready = signal("qkn_ready", ("PS",))
        mx_ready = signal("mx_ready", ("NT",))
        hn2_ready = signal("hn2_ready", ("OP",))
        gexp_ready = signal("gexp_ready", ("G",))
        gmax_ready = signal("gmax_ready", ("G",))
        hw_ready = signal("hw_ready", ("G",))
        qk2b_ready = signal("qk2b_ready", ("QK2",))
        mx2_ready = signal("mx2_ready", ("NT2",))
        res_ready = rd_sig["OP2"]
        rr_ready = signal("rr_ready", ("PS",))
        rinv_ready = signal("rinv_ready", ("PV",))
        sums2_ready = signal("sums2_ready", ("PV2",))
        rinv2_ready = signal("rinv2_ready", ("PV2",))
        norms = []
        for k, s, i in SCHED:
            norms += [(k, s, j) for j in range({"EMB": 3, "OP": 1}.get(k, 0))]
        var_ready, rstd_ready = ("var_ready", sem("var_ready")), ("rstd_ready", sem("rstd_ready"))
        steps["var_ready"] = steps["rstd_ready"] = norms
        x_loaded = [sem(f"x_loaded{s}") for s in range(2)]
        stored = [sem(f"stored{s}") for s in range(2)]
        consts_loaded = sem("consts_loaded")
        fills = sem("fills")
        setup_pe, setup_dve = sem("setup_pe"), sem("setup_dve")
        dve_chain, act_chain, pool_chain = sem("dve_chain"), sem("act_chain"), sem("pool_chain")

        def wait(eng, it, sig, p):
            n = steps[sig[0]]
            eng.wait_ge(sig[1], it * len(n) + n.index(p) + 1)

        def wait_earlier(eng, it, sig):
            eng.wait_ge(sig[1], it * len(steps[sig[0]]))

        loads = [(emb_raw, w_emb), (ln1_sb, ln1), (ln1b_sb, ln1_bias), (tokc, tok_const), (qk_w, w_qk),
                 (v_w, w_v), (out_w, w_out), (gl_w, w_gl), (qkv2_w, w_qkv2), (lorab_w, w_lora_b),
                 (bias2_w, w_bias2), (proj_w, w_proj), (scale_sb, scale), (rowc, row_const),
                 (mats_sb, mats), (sel_f, sel)]
        e_order = [p for p in SCHED if p[0] in ("ST", "ST2")]
        pv_order, pv2_order = steps["made_PV"], steps["made_PV2"]

        def wait_use(eng, it, kind, p):
            order = steps["made_" + kind]
            n = order.index(p)
            if n >= 2:
                wait(eng, it, rd_sig[kind], order[n - 2])
            else:
                wait_earlier(eng, it, rd_sig[kind])

        def tile_cols(t):
            return slice(TO * t, TO * t + TR)

        def key_rows(t):
            return TO if t == 0 else TR

        NFILLS = 16

        block = ctx.enter_context(nc.Block())

        @block.sync
        def _(sp):
            for dst, src in loads:
                sp.dma_start(dst[tuple(slice(None) for _ in src.shape)], src).then_inc(consts_loaded, 16)

            def load(it, s):
                sp.dma_start(xb[s][:], x_t[bass.ds(it * 2 + s, 1)].rearrange("b p c t -> (b p) c t")
                             ).then_inc(x_loaded[s], 16)

            def store(it, s):
                wait(sp, it, res_ready, ("OP2", s, 0))
                dst = out[bass.ds(it * 2 + s, 1)].rearrange("b t d -> (b t) d")
                sp.dma_start(dst[1:1 + TO], res[s][0:TO, 0, :]).then_inc(stored[s], 16)
                sp.dma_start(dst[1 + TO:NT], res[s][0:TO, 1, :]).then_inc(stored[s], 16)
                sp.dma_start(dst[0:1], res[s][TO:TR, 1, :]).then_inc(stored[s], 16)

            for s in range(2):
                load(0, s)
            with sp.Fori(0, ITERS - 1) as it:
                for s in range(2):
                    wait(sp, it, pe_sig["EMB"], ("EMB", s, 0))
                    wait(sp, it, xsq_ready, ("EMB", s, 0))
                    load(it + 1, s)
                for s in range(2):
                    store(it, s)
            for s in range(2):
                store(ITERS - 1, s)
            for s in range(2):
                sp.wait_ge(stored[s], 48 * ITERS)

        @block.gpsimd
        def _(pool):
            nc.gpsimd.memset(ones[:], 1.0).then_inc(fills, 1)
            nc.gpsimd.memset(emb_w[:, :, D:D + 1], 1.0).then_inc(fills, 1)
            for s in range(2):
                nc.gpsimd.memset(vx[s][:, :, :, DH:2 * DH], 1.0).then_inc(fills, 1)
                nc.gpsimd.memset(v2[s][:, :, :, DH2:2 * DH2], 1.0).then_inc(fills, 1)
                nc.gpsimd.memset(gates[s][:, :, NE:16], -1.0).then_inc(fills, 1)
                nc.gpsimd.memset(neg[s][:], 0.0).then_inc(fills, 1)
                nc.gpsimd.memset(comb[s][:, :, NE:NE + 1], 1.0).then_inc(fills, 1)
            nc.gpsimd.memset(half_neg[:], -0.5).then_inc(fills, 1)
            nc.gpsimd.memset(eps_ln[:], EPS).then_inc(fills, 1)
            nc.gpsimd.memset(tiny[:], 2.0 ** -62).then_inc(fills, 1)
            nc.gpsimd.memset(eps_qk[:], 1e-8).then_inc(fills, 1)
            pool.wait_ge(fills, NFILLS)
            with pool.Fori(0, ITERS) as it:
                for n, p in enumerate(norms):
                    wait(pool, it, var_ready, p)
                    nc.gpsimd.tensor_tensor(veps[:], mv[:, :, 1], eps_ln[:], ALU.add).then_inc(pool_chain, 1)
                    pool.wait_ge(pool_chain, it * len(norms) + n + 1)
                    nc.gpsimd.tensor_tensor(rstd[:], veps[:], half_neg[:], ALU.pow).then_inc(rstd_ready[1], 1)

        @block.tensor
        def _(pe):
            pe.wait_ge(consts_loaded, 16 * len(loads))
            pe.wait_ge(fills, NFILLS)
            pe.wait_ge(setup_dve, 1)
            for c in range(KC):
                nc.tensor.matmul(psum[0:TR, 0, 0:D], ones[:], emb_w[:, c, 0:D],
                                 start=(c == 0), stop=(c == KC - 1))
            for c in range(KC):
                mm = nc.tensor.matmul(psum[0:TR, 1, 0:D], ln1b_sb[:, c, :], emb_raw[:, c, :],
                                      start=(c == 0), stop=(c == KC - 1))
            mm.then_inc(setup_pe, 1)
            pe.wait_ge(setup_dve, 2)

            def ps(p, rows, cols, b=0):
                return psum[rows, bank[p] + b, cols]

            def transposes(p, src, width):
                for t in range(2):
                    n = key_rows(t)
                    last_mm = nc.tensor.transpose(ps(p, slice(0, width), slice(TO * t, TO * t + n)),
                                                  src(t, n), ident[0:n, 0:n])
                return last_mm

            def hidden_transposed(p, src):
                for c in range(2):
                    for t in range(2):
                        n = key_rows(t)
                        at = NT * c + TO * t
                        mm = nc.tensor.transpose(ps(p, slice(0, HC), slice(at, at + n)),
                                                 src[0:n, t, HC * c:HC * c + HC], ident[0:n, 0:n])
                return mm

            with pe.Fori(0, ITERS) as it:
                for p in SCHED:
                    kind, s, i = p
                    if before[p]:
                        wait(pe, it, rd_sig[before[p][0]], before[p])
                    else:
                        wait_earlier(pe, it, rd_sig[last[bank[p]][0]])
                    if kind == "EMB":
                        pe.wait_ge(x_loaded[s], it * 16 + 16)
                        for t in range(2):
                            for c in range(KC):
                                nc.tensor.matmul(ps(p, slice(0, TR), slice(194 * t, 194 * t + D + 1)),
                                                 xb[s][:, c, tile_cols(t)], emb_w[:, c, :],
                                                 start=(c == 0), stop=(c == KC - 1))
                        wait(pe, it, xss_ready, p)
                        for t in range(2):
                            mm = nc.tensor.matmul(ps(p, slice(0, TR), slice(194 * t + 193, 194 * t + 194)),
                                                  xss[s][:, tile_cols(t)], ones[:, 0:1],
                                                  start=True, stop=True)
                    elif kind == "T1":
                        wait(pe, it, hn_ready, ("EMB", s, 0))
                        mm = hidden_transposed(p, hn[s])
                    elif kind == "QK":
                        wait(pe, it, rd_sig["T1"], ("T1", s, 0))
                        for m in range(4):
                            for c in range(2):
                                f = 128 * (4 * i + m)
                                at = NT * (m % 2)
                                mm = nc.tensor.matmul(ps(p, slice(0, 128), slice(at, at + NT), m // 2),
                                                      qk_w[:, c, f:f + 128], hn_t[s][:, c, :],
                                                      start=(c == 0), stop=(c == 1))
                    elif kind == "PS":
                        wait(pe, it, ss_ready, p)
                        mm = nc.tensor.matmul(ps(p, slice(0, 128), slice(0, 2 * NT)), pair_sum,
                                              ss[s][:].rearrange("p a t -> p (a t)"), start=True, stop=True)
                    elif kind == "V":
                        for b in range(2):
                            for c in range(2):
                                mm = nc.tensor.matmul(ps(p, slice(0, TR), slice(0, INNER // 2), b),
                                                      hn_t[s][:, c, tile_cols(i)],
                                                      v_w[:, c, INNER // 2 * b:INNER // 2 * (b + 1)],
                                                      start=(c == 0), stop=(c == 1))
                    elif kind == "SM":
                        wait(pe, it, qkn_ready, ("PS", s, 0))
                        for e in range(2):
                            r = slice(DH * e, DH * e + DH)
                            for t in range(2):
                                mm = nc.tensor.matmul(ps(p, slice(0, TR), slice(NT * t, NT * t + NT), e),
                                                      qk_b[s][r, i, tile_cols(t)], qk_b[s][r, 6 + i, :],
                                                      start=True, stop=True)
                    elif kind in ("NT", "NT2"):
                        wait(pe, it, mx_ready if kind == "NT" else mx2_ready, p)
                        mm = transposes(p, lambda t, n: neg[s][0:n, t].rearrange("p a b -> p (a b)"), 128)
                    elif kind == "ST":
                        wait(pe, it, rd_sig["NT"], ("NT", s, 0))
                        for e in range(2):
                            r = slice(DH * e, DH * e + DH)
                            for t in range(2):
                                o = ps(p, slice(0, TR), slice(NT * t, NT * t + NT), e)
                                nc.tensor.matmul(o, sel_b[r, 0, 2 * i + e, :], neg_t[s][r, :], start=True, stop=False)
                                mm = nc.tensor.matmul(o, qk[s][r, 6 + i, tile_cols(t)], qk[s][r, i, :],
                                                      start=False, stop=True)
                    elif kind == "PV":
                        wait(pe, it, rd_sig["ST"], ("ST", s, i))
                        wait(pe, it, rd_sig["V"], ("V", s, 1))
                        eb = ebuf[e_order.index(("ST", s, i)) % EBUFS]
                        for e in range(2):
                            for t in range(2):
                                n = key_rows(t)
                                mm = nc.tensor.matmul(ps(p, slice(0, 128), slice(NT * e, NT * e + NT)),
                                                      vx[s][0:n, t, 2 * i + e, :], eb[0:n, e, t, :],
                                                      start=(t == 0), stop=(t == 1))
                    elif kind == "OP":
                        wait(pe, it, rd_sig["PV"], ("PV", s, 5))
                        for t in range(2):
                            for m in range(H // 2):
                                mm = nc.tensor.matmul(ps(p, slice(0, TR), slice(D * t, D * t + D)),
                                                      o_t[s][:, m, tile_cols(t)], out_w[:, m, :],
                                                      start=(m == 0), stop=(m == H // 2 - 1))
                    elif kind == "T2":
                        wait(pe, it, hn2_ready, ("OP", s, 0))
                        mm = hidden_transposed(p, hn[s])
                    elif kind == "G":
                        wait(pe, it, rd_sig["T2"], ("T2", s, 0))
                        for t in range(2):
                            for c in range(2):
                                mm = nc.tensor.matmul(ps(p, slice(0, TR), slice(136 * t, 136 * t + 136)),
                                                      hn2_t[s][:, c, tile_cols(t)], gl_w[:, c, :],
                                                      start=(c == 0), stop=(c == 1))
                    elif kind == "T3":
                        wait(pe, it, hw_ready, ("G", s, 0))
                        transposes(p, lambda t, n: hw[s][0:n, t].rearrange("p e r -> p (e r)"), 128)
                        for t in range(2):
                            n = key_rows(t)
                            mm = nc.tensor.transpose(ps(p, slice(0, NE + 1), slice(NT + TO * t, NT + TO * t + n)),
                                                     comb[s][0:n, t, :], ident[0:n, 0:n])
                    elif kind == "QK2":
                        wait(pe, it, rd_sig["T3"], ("T3", s, 0))
                        for m in range(3):
                            o = ps(p, slice(0, 128), slice(NT * (m % 2), NT * (m % 2) + NT), m // 2)
                            f = slice(128 * m, 128 * m + 128)
                            for c in range(2):
                                nc.tensor.matmul(o, qkv2_w[:, c, f], hn2_t[s][:, c, :],
                                                 start=(c == 0), stop=False)
                            nc.tensor.matmul(o, lorab_w[:, f], hw_t[s][:], start=False, stop=False)
                            mm = nc.tensor.matmul(o, bias2_w[:, f], comb_t[s][:], start=False, stop=True)
                    elif kind == "V2":
                        for t in range(2):
                            o = ps(p, slice(0, TR), slice(D * t, D * t + D))
                            f = slice(2 * D, 3 * D)
                            for c in range(2):
                                nc.tensor.matmul(o, hn2_t[s][:, c, tile_cols(t)], qkv2_w[:, c, f],
                                                 start=(c == 0), stop=False)
                            nc.tensor.matmul(o, hw_t[s][:, tile_cols(t)], lorab_w[:, f], start=False, stop=False)
                            mm = nc.tensor.matmul(o, comb_t[s][:, tile_cols(t)], bias2_w[:, f],
                                                  start=False, stop=True)
                    elif kind in ("SM2", "ST2"):
                        g, r = i // 4, slice(32 * (i % 4), 32 * (i % 4) + 32)
                        if kind == "SM2":
                            wait(pe, it, qk2b_ready, ("QK2", s, 0))
                        else:
                            wait(pe, it, rd_sig["NT2"], ("NT2", s, 0))
                        for e in range(2):
                            for t in range(2):
                                o = ps(p, slice(0, TR), slice(NT * t, NT * t + NT), e)
                                if kind == "SM2":
                                    mm = nc.tensor.matmul(o, q2b[s][r, g, tile_cols(t)], k2b[s][r, g, e, :],
                                                          start=True, stop=True)
                                else:
                                    nc.tensor.matmul(o, sel_b[r, 1, 2 * i + e, :], neg_t[s][r, :],
                                                     start=True, stop=False)
                                    mm = nc.tensor.matmul(o, k2[s][r, g, e, tile_cols(t)], q2[s][r, g, :],
                                                          start=False, stop=True)
                    elif kind == "PV2":
                        wait(pe, it, rd_sig["ST2"], ("ST2", s, 2 * i + 1))
                        wait(pe, it, rd_sig["V2"], ("V2", s, 0))
                        for t in range(2):
                            n = key_rows(t)
                            for j in range(4):
                                eb = ebuf[e_order.index(("ST2", s, 2 * i + j // 2)) % EBUFS]
                                mm = nc.tensor.matmul(ps(p, slice(32 * j, 32 * j + 32), slice(0, NT)),
                                                      v2[s][0:n, t, 4 * i + j, :], eb[0:n, j % 2, t, :],
                                                      start=(t == 0), stop=(t == 1))
                    elif kind == "OP2":
                        wait(pe, it, rd_sig["PV2"], ("PV2", s, 2))
                        for t in range(2):
                            for m in range(3):
                                mm = nc.tensor.matmul(ps(p, slice(0, TR), slice(D * t, D * t + D)),
                                                      o2_t[s][:, m, tile_cols(t)], proj_w[:, m, :],
                                                      start=(m == 0), stop=(m == 2))
                    mm.then_inc(pe_sig[kind][1], 1)

        @block.scalar
        def _(act):
            act.wait_ge(consts_loaded, 16 * len(loads))
            act.wait_ge(fills, NFILLS)
            act.wait_ge(setup_dve, 2)
            nc.scalar.preload_act_table_set("natural_log_exp_and_others")
            count = [0]

            def link(ins):
                count[0] += 1
                ins.then_inc(act_chain, 1)
                act.wait_ge(act_chain, count[0])

            with act.Fori(0, ITERS) as it:
                act.sem_clear(act_chain)
                count[0] = 0
                for p in SCHED:
                    kind, s, i = p
                    done = rd_sig[kind][1] if kind in rd_sig else None
                    b = bank[p]
                    if kind == "EMB":
                        act.wait_ge(x_loaded[s], it * 16 + 16)
                        if s == 0:
                            wait_earlier(act, it, ss_ready)
                        else:
                            wait(act, it, xss_ready, ("EMB", 0, 0))
                        nc.scalar.activation(xsq, xb[s][:], ACT.Square).then_inc(xsq_ready[1], 1)
                    elif kind in ("T1", "T2"):
                        wait(act, it, pe_sig[kind], p)
                        dst = hn_t if kind == "T1" else hn2_t
                        nc.scalar.copy(dst[s][:].rearrange("p c t -> p (c t)"),
                                       psum[0:HC, b, 0:2 * NT]).then_inc(done, 1)
                    elif kind == "QK":
                        wait(act, it, pe_sig[kind], p)
                        src = psum[:, b:b + 2, 0:2 * NT]
                        if i == 0:
                            if s == 0:
                                wait(act, it, xss_ready, ("EMB", 1, 0))
                            else:
                                wait(act, it, ss_ready, ("PS", 0, 0))
                        nc.scalar.activation(
                            qk_sq[:, 4 * i:4 * i + 4, :].rearrange("p (b m) t -> p b (m t)", b=2),
                            src, ACT.Square)
                        nc.scalar.copy(qk[s][:, 4 * i:4 * i + 4, :].rearrange("p (b m) t -> p b (m t)", b=2),
                                       src).then_inc(done, 1)
                    elif kind == "PS":
                        wait(act, it, pe_sig[kind], p)
                        n2 = nrm[s][:]
                        nc.scalar.activation(n2, psum[:, b, 0:2 * NT], ACT.Ln, bias=tiny[:]).then_inc(done, 1)
                        wait(act, it, rd_sig[kind], p)
                        link(nc.scalar.activation(n2, n2, ACT.Exp, scale=0.5))
                        link(nc.scalar.activation(n2, n2, ACT.Ln, bias=eps_qk[:]))
                        nc.scalar.activation(n2, n2, ACT.Exp, scale=-0.5).then_inc(rr_ready[1], 1)
                    elif kind == "V":
                        wait(act, it, pe_sig[kind], p)
                        nc.scalar.copy(
                            vx[s][:, i, :, 0:DH].rearrange("p (b h) d -> p b h d", b=2),
                            psum[0:TR, b:b + 2, 0:INNER // 2].rearrange("p b (h d) -> p b h d", d=DH)
                        ).then_inc(done, 1)
                    elif kind in ("NT", "NT2"):
                        wait(act, it, pe_sig[kind], p)
                        nc.scalar.copy(neg_t[s][:], psum[:, b, 0:NT]).then_inc(done, 1)
                    elif kind in ("ST", "ST2"):
                        wait(act, it, pe_sig[kind], p)
                        n = e_order.index(p)
                        if n >= EBUFS:
                            k0, s0, i0 = e_order[n - EBUFS]
                            user = ("PV", s0, i0) if k0 == "ST" else ("PV2", s0, i0 // 2)
                            wait(act, it, pe_sig[user[0]], user)
                        else:
                            wait_earlier(act, it, pe_sig["PV2"])
                        nc.scalar.activation(ebuf[n % EBUFS][:].rearrange("p e a t -> p e (a t)"),
                                             psum[0:TR, b:b + 2, 0:2 * NT], ACT.Exp).then_inc(done, 1)
                    elif kind == "PV":
                        wait(act, it, pe_sig[kind], p)
                        wait_use(act, it, "PV", p)
                        r = rinv[pv_order.index(p) % 2][:]
                        link(nc.scalar.activation(r, psum[DH:128, b, 0:2 * NT], ACT.Ln))
                        nc.scalar.activation(r, r, ACT.Exp, scale=-1.0).then_inc(rinv_ready[1], 1)
                    elif kind == "PV2":
                        wait(act, it, sums2_ready, p)
                        r = sums2[pv2_order.index(p) % 2][:]
                        link(nc.scalar.activation(r, r, ACT.Ln))
                        nc.scalar.activation(r, r, ACT.Exp, scale=-1.0).then_inc(rinv2_ready[1], 1)
                    elif kind == "G":
                        wait(act, it, gmax_ready, p)
                        nc.scalar.activation(gates[s][:, :, 0:NE], gl[s][:, :, 0:NE], ACT.Exp
                                             ).then_inc(gexp_ready[1], 1)
                    elif kind == "T3":
                        wait(act, it, pe_sig[kind], p)
                        nc.scalar.copy(hw_t[s][:], psum[:, b, 0:NT])
                        nc.scalar.copy(comb_t[s][:], psum[0:NE + 1, b, NT:2 * NT]).then_inc(done, 1)
                    elif kind == "QK2":
                        wait(act, it, pe_sig[kind], p)
                        nc.scalar.mul(q2[s][:, 0, :], psum[:, b, 0:NT], QSCALE)
                        nc.scalar.mul(q2[s][0:64, 1, :], psum[0:64, b + 1, 0:NT], QSCALE)
                        for e in range(2):
                            nc.scalar.activation(k2[s][:, 0, e, :], psum[:, b, NT:2 * NT], ACT.Copy,
                                                 scale=parity[e])
                            a = nc.scalar.activation(k2[s][0:64, 1, e, :], psum[64:128, b + 1, 0:NT], ACT.Copy,
                                                     scale=parity[e][64:128])
                        a.then_inc(done, 1)
                    elif kind == "V2":
                        wait(act, it, pe_sig[kind], p)
                        nc.scalar.copy(v2[s][:, :, :, 0:DH2],
                                       psum[0:TR, b, 0:2 * D].rearrange("p (a h d) -> p a h d", a=2, d=DH2)
                                       ).then_inc(done, 1)

        @block.vector
        def _(dve):
            count = [0]

            def link(ins):
                count[0] += 1
                ins.then_inc(dve_chain, 1)
                dve.wait_ge(dve_chain, count[0])

            dve.wait_ge(consts_loaded, 16 * len(loads))
            dve.wait_ge(fills, NFILLS)
            nc.vector.tensor_tensor(emb_w[:, :, 0:D], emb_raw,
                                    ln1_sb[:].unsqueeze(2).broadcast_to([128, KC, D]), ALU.mult
                                    ).then_inc(setup_dve, 1)
            nc.vector.reciprocal(inv_scale[:], scale_sb[:])
            nc.vector.tensor_copy(sel_b[:], sel_f.unsqueeze(3).broadcast_to([128, 2, H, TR]))
            dve.wait_ge(setup_pe, 1)
            nc.vector.tensor_copy(emb_cs[:], psum[0:TR, 0, 0:D])
            nc.vector.tensor_tensor(emb_b[:], tokc[:, 2, 0, :], psum[0:TR, 1, 0:D], ALU.add
                                    ).then_inc(setup_dve, 1)
            dve.wait_ge(setup_dve, 2)

            def inverse_std(p):
                wait(dve, it, rstd_ready, p)

            def layernorm(p, src, dst, sig=None):
                for t in range(2):
                    a = nc.vector.bn_stats(st6[:, t, :], src[:, t, :])
                link(a)
                for t in range(2):
                    a = nc.vector.bn_aggr(mv[:, t, :], st6[:, t, :])
                a.then_inc(var_ready[1], 1)
                inverse_std(p)
                for t in range(2):
                    a = nc.vector.tensor_scalar(dst[:, t, :], src[:, t, :], mv[:, t, 0:1], rstd[:, t:t + 1],
                                                ALU.subtract, ALU.mult)
                if sig is None:
                    link(a)
                else:
                    a.then_inc(sig[1], 1)

            with dve.Fori(0, ITERS) as it:
                dve.sem_clear(dve_chain)
                count[0] = 0
                for p in SCHED:
                    kind, s, i = p
                    done = rd_sig[kind][1] if kind in rd_sig else None
                    b = bank[p]
                    if kind == "EMB":
                        wait(dve, it, xsq_ready, p)
                        nc.vector.tensor_reduce(xss[s][:], xsq.rearrange("p c t -> p t c"), AX.X, ALU.add
                                                ).then_inc(xss_ready[1], 1)
                        wait(dve, it, pe_sig[kind], p)
                        sums = psum[0:TR, b, 0:388].rearrange("p (t f) -> p t f", t=2)
                        link(nc.vector.tensor_scalar(nmean[:], sums[:, :, D], -1.0 / PD, None, ALU.mult))
                        link(nc.vector.tensor_tensor(msq[:], nmean[:], nmean[:], ALU.mult))
                        nc.vector.scalar_tensor_tensor(out=mv[:, :, 1], in0=sums[:, :, D + 1], scalar=1.0 / PD,
                                                            in1=msq[:], op0=ALU.mult, op1=ALU.subtract
                                                            ).then_inc(var_ready[1], 1)
                        inverse_std(("EMB", s, 0))
                        for t in range(2):
                            a = nc.vector.scalar_tensor_tensor(out=lnt[:, t, :], in0=emb_cs[:],
                                                               scalar=nmean[:, t:t + 1], in1=sums[:, t, 0:D],
                                                               op0=ALU.mult, op1=ALU.add)
                        a.then_inc(done, 1)
                        wait(dve, it, rd_sig[kind], p)
                        for t in range(2):
                            a = nc.vector.scalar_tensor_tensor(out=lnt[:, t, :], in0=lnt[:, t, :],
                                                               scalar=rstd[:, t:t + 1], in1=emb_b[:],
                                                               op0=ALU.mult, op1=ALU.add)
                        link(a)
                        layernorm(("EMB", s, 1), lnt, h0[s])
                        link(nc.vector.tensor_tensor(h0[s][:], h0[s][:], tokc[:, 0], ALU.mult))
                        link(nc.vector.tensor_tensor(h0[s][:], h0[s][:], tokc[:, 1], ALU.add))
                        layernorm(("EMB", s, 2), h0[s], hn[s], hn_ready)
                        wait(dve, it, hn_ready, p)
                        link(nc.vector.tensor_tensor(h0[s][:], h0[s][:],
                                                     b_out.unsqueeze(1).broadcast_to([TR, 2, D]), ALU.add))
                    elif kind == "PS":
                        wait(dve, it, rd_sig["QK"], ("QK", s, 2))
                        for a in range(2):
                            r = nc.vector.tensor_reduce(ss[s][:, a, :],
                                                        qk_sq[:, 6 * a:6 * a + 6, :].rearrange("p m t -> p t m"),
                                                        AX.X, ALU.add)
                        r.then_inc(ss_ready[1], 1)
                        wait(dve, it, rr_ready, p)
                        for m in range(6):
                            nc.vector.scalar_tensor_tensor(out=qk[s][:, m, :], in0=qk[s][:, m, :],
                                                           scalar=inv_scale[:, m:m + 1], in1=nrm[s][:, 0:NT],
                                                           op0=ALU.mult, op1=ALU.mult)
                        link(nc.vector.tensor_tensor(qk[s][:, 6:12, :], qk[s][:, 6:12, :],
                                                     nrm[s][:, NT:2 * NT].unsqueeze(1).broadcast_to([128, 6, NT]), ALU.mult))
                        nc.vector.tensor_copy(qk_b[s][:], qk[s][:]).then_inc(qkn_ready[1], 1)
                    elif kind in ("SM", "SM2"):
                        wait(dve, it, pe_sig[kind], p)
                        nc.vector.tensor_reduce(
                            mx[s][:, :, 2 * i:2 * i + 2].rearrange("p a e -> p e a"),
                            psum[0:TR, b:b + 2, 0:2 * NT].rearrange("p e (a t) -> p e a t", a=2),
                            AX.X, ALU.max).then_inc(done, 1)
                        if i == 5:
                            wait(dve, it, rd_sig[kind], p)
                            ready = mx_ready if kind == "SM" else mx2_ready
                            nc.vector.tensor_scalar(neg[s][:, :, :, 0:H],
                                                    mx[s][:].unsqueeze(2).broadcast_to([TR, 2, 4, H]),
                                                    -1.0, None, ALU.mult).then_inc(ready[1], 1)
                    elif kind == "PV":
                        wait(dve, it, rinv_ready, p)
                        r = rinv[pv_order.index(p) % 2]
                        for e in range(2):
                            a = nc.vector.tensor_tensor(o_t[s][DH * e:DH * e + DH, i, :],
                                                        psum[0:DH, b, NT * e:NT * e + NT],
                                                        r[:, NT * e:NT * e + NT], ALU.mult)
                        a.then_inc(done, 1)
                    elif kind == "OP":
                        dve.wait_ge(stored[s], it * 48)
                        wait(dve, it, pe_sig[kind], p)
                        nc.vector.tensor_tensor(h1[s][:].rearrange("p a d -> p (a d)"), psum[0:TR, b, 0:2 * D],
                                                h0[s][:].rearrange("p a d -> p (a d)"), ALU.add).then_inc(done, 1)
                        wait(dve, it, rd_sig[kind], p)
                        layernorm(("OP", s, 0), h1[s], hn[s], hn2_ready)
                        wait(dve, it, hn2_ready, p)
                        link(nc.vector.tensor_tensor(h1[s][:], h1[s][:],
                                                     b_proj.unsqueeze(1).broadcast_to([TR, 2, D]), ALU.add))
                    elif kind == "G":
                        wait(dve, it, pe_sig[kind], p)
                        nc.vector.tensor_tensor(gl[s][:], psum[0:TR, b, 0:272].rearrange("p (t f) -> p t f", t=2),
                                                b_gl.unsqueeze(1).broadcast_to([TR, 2, 136]), ALU.add
                                                ).then_inc(done, 1)
                        wait(dve, it, rd_sig[kind], p)
                        link(nc.vector.tensor_reduce(gmax[:], gl[s][:, :, 0:NE], AX.X, ALU.max))
                        nc.vector.tensor_tensor(gl[s][:, :, 0:NE], gl[s][:, :, 0:NE],
                                                gmax[:].unsqueeze(2).broadcast_to([TR, 2, NE]), ALU.subtract
                                                ).then_inc(gmax_ready[1], 1)
                        wait(dve, it, gexp_ready, p)
                        link(nc.vector.tensor_reduce(gsum[:], gates[s][:, :, 0:NE], AX.X, ALU.add))
                        link(nc.vector.reciprocal(gsum[:], gsum[:]))
                        link(nc.vector.tensor_scalar(gsum[:], gsum[:], LORA_SCALE, None, ALU.mult))
                        for t in range(2):
                            a = nc.vector.max(top8[:, t, :], gates[s][:, t, :])
                        link(a)
                        link(nc.vector.memset(top8[:, :, 2:8], -1.0))
                        for t in range(2):
                            a = nc.vector.match_replace(rest[:, t, :], top8[:, t, :], gates[s][:, t, :], 0.0)
                        link(a)
                        link(nc.vector.tensor_tensor(rest[:, :, 0:NE], gates[s][:, :, 0:NE], rest[:, :, 0:NE],
                                                     ALU.subtract))
                        link(nc.vector.tensor_tensor(comb[s][:, :, 0:NE], rest[:, :, 0:NE],
                                                     gsum[:].unsqueeze(2).broadcast_to([TR, 2, NE]), ALU.mult))
                        for t in range(2):
                            a = nc.vector.tensor_tensor(
                                hw[s][:, t], gl[s][:, t, NE:].rearrange("p (e r) -> p e r", e=NE),
                                comb[s][:, t, 0:NE].unsqueeze(2).broadcast_to([TR, NE, RANK]), ALU.mult)
                        a.then_inc(hw_ready[1], 1)
                    elif kind == "QK2":
                        wait(dve, it, rd_sig[kind], p)
                        nc.vector.tensor_copy(q2b[s][:, 0, :], q2[s][:, 0, :])
                        nc.vector.tensor_copy(q2b[s][0:64, 1, :], q2[s][0:64, 1, :])
                        nc.vector.tensor_copy(k2b[s][:, 0], k2[s][:, 0])
                        nc.vector.tensor_copy(k2b[s][0:64, 1], k2[s][0:64, 1]).then_inc(qk2b_ready[1], 1)
                    elif kind == "PV2":
                        wait(dve, it, pe_sig[kind], p)
                        o = o2_t[s][:, i, :]
                        link(nc.vector.tensor_copy(o, psum[:, b, 0:NT]))
                        r = sums2[pv2_order.index(p) % 2]
                        nc.vector.stream_shuffle(r[:], o, [j + 16 if j < 16 else j for j in range(32)]
                                                 ).then_inc(sums2_ready[1], 1)
                        wait(dve, it, rinv2_ready, p)
                        nc.vector.tensor_tensor(o, o, r[:], ALU.mult).then_inc(done, 1)
                    elif kind == "OP2":
                        wait(dve, it, pe_sig[kind], p)
                        nc.vector.tensor_tensor(res[s][:].rearrange("p a d -> p (a d)"), psum[0:TR, b, 0:2 * D],
                                                h1[s][:].rearrange("p a d -> p (a d)"), ALU.add
                                                ).then_inc(done, 1)


def kernel(x, L0_tok_ln1_g, L0_tok_ln1_b, L0_tok_W, L0_tok_b, L0_tok_ln2_g, L0_tok_ln2_b, L0_tok_cls,
           L0_attn_w_qkv, L0_attn_w_out, L0_attn_b_out, L0_attn_scale, L0_ffn_Wg, L0_ffn_bg, L0_ffn_Wqkv,
           L0_ffn_bqkv, L0_ffn_Wproj, L0_ffn_bproj, L0_ffn_A, L0_ffn_ba, L0_ffn_Bm, L0_ffn_bb):
    import concourse.bacc as bacc
    from concourse.bass_utils import run_bass_kernel_spmd

    f = np.float32
    p = np.asarray(x).reshape(B, 3, 14, 16, 14, 16).transpose(0, 3, 5, 1, 2, 4).reshape(B, KC, 128, NP)
    x_t = np.zeros((B, 128, KC, NT), f)
    x_t[..., :NP] = p.transpose(0, 2, 1, 3)

    def chunks(a, rows):
        a = np.asarray(a)
        return a.reshape(-1, rows, a.shape[-1]).transpose(1, 0, 2)

    ln1 = chunks(np.asarray(L0_tok_ln1_g).reshape(PD, 1), 128)[:, :, 0]
    ln1_bias = np.repeat(chunks(np.asarray(L0_tok_ln1_b).reshape(PD, 1), 128), TR, axis=2)
    tok_const = np.zeros((TR, 3, 2, D), f)
    tok_const[:, 0], tok_const[:, 1], tok_const[:, 2] = L0_tok_ln2_g, L0_tok_ln2_b, L0_tok_b
    tok_const[TR - 1, 0, 1] = 0
    tok_const[TR - 1, 1, 1] = np.asarray(L0_tok_cls)[0, 0]
    w_t = np.asarray(L0_attn_w_qkv).T
    w2 = np.asarray(L0_ffn_Wqkv).T
    order = np.r_[0:128, D:D + 128, 128:D, D + 128:2 * D, 2 * D:3 * D]
    w_gl = np.concatenate([np.asarray(L0_ffn_Wg), np.asarray(L0_ffn_A).reshape(NE * RANK, D)]).T
    w_lora_b = np.asarray(L0_ffn_Bm).transpose(0, 2, 1).reshape(NE * RANK, 3 * D)[:, order]
    w_bias2 = np.concatenate([np.asarray(L0_ffn_bb), np.asarray(L0_ffn_bqkv)[None]])[:, order]
    w_proj = np.zeros((3, 4, 32, D), f)
    w_proj[:, :, :DH2] = np.asarray(L0_ffn_Wproj).T.reshape(3, 4, DH2, D)
    scale = np.repeat(np.asarray(L0_attn_scale).reshape(H // 2, 2), DH, axis=1).T
    row = np.concatenate([np.asarray(L0_attn_b_out), np.asarray(L0_ffn_bproj), np.asarray(L0_ffn_bg),
                          np.asarray(L0_ffn_ba).reshape(-1)])
    row_const = np.repeat(row[None], TR, axis=0)
    mats = np.zeros((128, 258), f)
    r = np.arange(128)
    mats[r, r] = 1
    mats[:, 128:256] = (r[:, None] % DH == r[None, :] % DH)
    mats[:, 256], mats[:, 257] = r % 32 < 16, r % 32 >= 16
    sel = np.zeros((128, 2, H), f)
    for h in range(H):
        sel[[h, 64 + h], 0, h] = 1
        sel[[h, 32 + h, 64 + h, 96 + h], 1, h] = 1

    arrays = {
        "x_t": x_t, "w_emb": chunks(L0_tok_W, 128), "ln1": ln1, "ln1_bias": ln1_bias, "tok_const": tok_const,
        "w_qk": chunks(w_t[:, :2 * INNER], HC), "w_v": chunks(w_t[:, 2 * INNER:], HC),
        "w_out": chunks(np.asarray(L0_attn_w_out).T, 128), "w_gl": chunks(w_gl, HC),
        "w_qkv2": chunks(w2[:, order], HC), "w_lora_b": w_lora_b, "w_bias2": w_bias2,
        "w_proj": chunks(w_proj.reshape(384, D), 128), "scale": scale, "row_const": row_const,
        "mats": mats, "sel": sel,
    }
    arrays = {k: np.ascontiguousarray(v) for k, v in arrays.items()}
    nc = bacc.Bacc("TRN2", target_bir_lowering=False, num_devices=1)
    args = [nc.dram_tensor(k, v.shape, mybir.dt.from_np(v.dtype), kind="ExternalInput").ap()
            for k, v in arrays.items()]
    out = nc.dram_tensor("out", (B, NT, D), mybir.dt.float32, kind="ExternalOutput").ap()
    vit_tower(nc, *args, out)
    return run_bass_kernel_spmd(nc, [arrays], core_ids=[0]).results[0]["out"]
```

```python
import numpy as np
import concourse.bass as bass
from concourse import mybir
from contextlib import ExitStack

B, D, NP = 64, 192, 196
NT = NP + 1
PD, KC = 768, 6
TR, TO = 99, 98
H, DH = 12, 64
DH2 = D // H
INNER = H * DH
NE, RANK = 8, 16
HC = D // 2
ITERS = B // 2
EPS = 1e-5
LORA_SCALE = 32 / RANK
NTP = NT + 1
G2 = 3
QKV2 = 2 * G2 * 128 + D
WS = 64.0
QSCALE = DH2 ** -0.5

SCHED = []
for kind, count in (("EMB", 1), ("T1", 1), ("QK", 3), ("PS", 1), ("V", 2), ("SM", 6), ("NT", 1),
                    ("ATT", 6), ("OP", 1), ("T2", 1), ("G", 1), ("T3", 1), ("QK2", 2), ("V2", 1),
                    ("SM2", 6), ("NT2", 1), ("ATT2", 6), ("OP2", 1)):
    for s in range(2):
        for i in range(count):
            if kind == "ATT":
                SCHED.append(("ST", s, i))
                if i >= 1:
                    SCHED.append(("PV", s, i - 1))
            elif kind == "ATT2":
                SCHED.append(("ST2", s, i))
                if i in (2, 4):
                    SCHED.append(("PV2", s, i // 2 - 1))
            else:
                SCHED.append((kind, s, i))
        if kind == "ATT":
            SCHED.append(("PV", s, 5))
        if kind == "ATT2":
            SCHED.append(("PV2", s, 2))
WIDE = ("QK", "V", "SM", "ST", "QK2", "SM2", "ST2")
EBUFS = 3


def place():
    bank, before, last, wide, narrow = {}, {}, {}, 0, 0
    for p in SCHED:
        if p[0] in WIDE:
            b, wide = 2 * (wide % 3), wide + 1
        else:
            b, narrow = 6 + narrow % 2, narrow + 1
        bank[p], before[p], last[b] = b, last.get(b), p
    return bank, before, last


def vit_tower(nc, x_t, w_emb, ln1, ln1_bias, tok_const, tok_bias, w_qk, w_v, w_out, w_gl, w_qkv2, w_lora_b,
              w_bias2, w_proj, scale, row_const, mats, sel, out):
    F32, F16 = mybir.dt.float32, mybir.dt.float16
    ALU, ACT, AX = mybir.AluOpType, mybir.ActivationFunctionType, mybir.AxisListType
    ctx = ExitStack()
    with ctx:
        def sb(name, shape, dt=F32):
            return ctx.enter_context(nc.sbuf_tensor(name, shape, dt))

        def two(name, shape, dt=F32):
            return [sb(f"{name}{s}", shape, dt) for s in range(2)]

        def sem(name):
            return ctx.enter_context(nc.semaphore(name))

        emb_w = sb("emb_w", [128, KC, D + 1])
        ln1_sb = sb("ln1_sb", [128, KC])
        tokc = sb("tokc", [TR, 2, 2, D])
        emb_cs = sb("emb_cs", [TR, D])
        emb_b = sb("emb_b", [TR, D])
        qk_w = sb("qk_w", [HC, 2, 2, 2 * INNER], F16)
        v_w = sb("v_w", [HC, 2, 2, INNER], F16)
        out_w = sb("out_w", [128, H // 2, D])
        gl_w = sb("gl_w", [HC, 2, NE + NE * RANK])
        qkv2_w = sb("qkv2_w", [HC, 2, 2, QKV2], F16)
        lorab_w = sb("lorab_w", [128, 2, QKV2], F16)
        bias2_w = sb("bias2_w", [3 * (NE + 1), QKV2], F16)
        proj_w = sb("proj_w", [128, 3, D])
        scale_sb = sb("scale_sb", [128, H // 2])
        inv_scale = sb("inv_scale", [128, H // 2])
        rowc = sb("rowc", [TR, 2 * D + NE + NE * RANK])
        mats_sb = sb("mats_sb", [128, 261])
        ident, pair_sum = mats_sb[:, 0:128], mats_sb[:, 128:256]
        masks = mats_sb[:, 256:260]
        low_row = mats_sb[0:3 * (NE + 1), 260:261]
        ones = sb("ones", [128, TR])
        b_out, b_proj = rowc[:, 0:D], rowc[:, D:2 * D]
        b_gl = rowc[:, 2 * D:]

        xb = two("xb", [128, KC, NT])
        xss = two("xss", [128, NT])
        h0, h1 = two("h0", [TR, 2, D]), two("h1", [TR, 2, D])
        hn = two("hn", [TR, 2, D])
        hn_s, hn2_s = two("hn_s", [HC, 2, 2, NTP], F16), two("hn2_s", [HC, 2, 2, NTP], F16)
        qk = two("qk", [128, H, NT])
        qk_sq = sb("qk_sq", [128, H, NT])
        xsq = qk_sq[:, 0:KC, :]
        qa, qb = two("qa", [128, H, NTP], F16), two("qb", [128, H, NTP], F16)
        ka, kb = two("ka", [128, H, NTP], F16), two("kb", [128, H, NTP], F16)
        high, low = sb("high", [128, H // 2, NTP], F16), sb("low", [128, H // 2, NTP], F16)
        ss = two("ss", [128, 2, NT])
        nrm = [ss[s][:].rearrange("p a t -> p (a t)") for s in range(2)]
        hn2_t = [ss[s][0:HC] for s in range(2)]
        vx = two("vx", [TR, 2, H, 2 * DH])
        mx = two("mx", [TR, 2, H])
        neg = two("neg", [TR, 2, 128])
        ebuf = [sb(f"ebuf{i}", [TR, 2, 2, NT]) for i in range(EBUFS)]
        rinv = two("rinv", [DH, 2 * NT])
        half_neg, eps_ln = sb("half_neg", [TR, 2]), sb("eps_ln", [TR, 2])
        tiny, eps_qk = sb("tiny", [128, 1]), sb("eps_qk", [128, 1])
        o_t = [qk[s][:, 0:H // 2, :] for s in range(2)]
        gl = two("gl", [TR, 2, NE + NE * RANK])
        gmax = sb("gmax", [TR, 2])
        gates = two("gates", [TR, 2, 16])
        top8 = sb("top8", [TR, 2, 8])
        rest = sb("rest", [TR, 2, 16])
        gsum = sb("gsum", [TR, 2])
        comb = two("comb", [TR, 2, NE + 1])
        comb_h = sb("comb_h", [TR, 2, NE + 1], F16)
        comb3 = two("comb3", [TR, 2, 3, NE + 1])
        hw = two("hw", [TR, 2, NE, RANK])
        hw_s = two("hw_s", [128, 2, NTP], F16)
        comb_t = two("comb_t", [3 * (NE + 1), NTP], F16)
        v2 = two("v2", [TR, 2, H, 2 * DH2])
        sums2 = two("sums2", [128, NT])
        o2_t = [qk[s][:, 6:9, :] for s in range(2)]
        res = h1
        st6 = sb("st6", [TR, 2, 6])
        mv = sb("mv", [TR, 2, 2])
        rstd = sb("rstd", [TR, 2])
        veps = sb("veps", [TR, 2])
        lnt = sb("lnt", [TR, 2, D])
        nmean = sb("nmean", [TR, 2])
        msq = sb("msq", [TR, 2])
        def flat(t, rows, first, *shape):
            n = int(np.prod(shape))
            names = "abc"[:len(shape)]
            return t[0:rows].rearrange("p a t -> p (a t)")[:, first:first + n].rearrange(
                f"p ({' '.join(names)}) -> p {' '.join(names)}", **dict(zip(names, shape)))

        emb_raw = flat(qk_sq, 128, 0, KC, D)
        ln1b_raw = flat(qk_sq, 128, KC * D, KC, TR)
        tok_b = flat(qk_sq, TR, KC * (D + TR) + H, 1, D)
        sel_raw = flat(qk_sq, 128, KC * (D + TR), H, 1)
        vx_flat = [vx[s][:].rearrange("p a h d -> p (a h) d") for s in range(2)]
        qk_raw = flat(vx_flat[0], HC, 0, 2, 2 * INNER)
        v_raw = flat(vx_flat[1], HC, 0, 2, INNER)
        qkv2_raw = flat(qk[0], HC, 0, 2, QKV2)
        lorab_raw = flat(qk[1], 128, 0, 1, QKV2)
        bias2_raw = flat(qk[1], 3 * (NE + 1), QKV2, 1, QKV2)

        psum = ctx.enter_context(nc.psum_tensor("psum", [128, 8, 512], F32))
        bank, before, last = place()

        steps = {}

        def signal(name, kinds):
            steps[name] = [p for p in SCHED if p[0] in kinds]
            return name, sem(name)

        pe_sig = {k: signal("made_" + k, (k,)) for k in
                  ("EMB", "T1", "QK", "PS", "V", "SM", "NT", "ST", "PV", "OP", "T2", "G", "T3",
                   "QK2", "V2", "SM2", "NT2", "ST2", "PV2", "OP2")}
        rd_sig = {k: signal("read_" + k, (k,)) for k in pe_sig}
        hn_ready = signal("hn_ready", ("EMB",))
        xss_ready = signal("xss_ready", ("EMB",))
        xsq_ready = signal("xsq_ready", ("EMB",))
        ss_ready = signal("ss_ready", ("PS",))
        qkn_ready = signal("qkn_ready", ("PS",))
        mx_ready = signal("mx_ready", ("NT",))
        hn2_ready = signal("hn2_ready", ("OP",))
        gexp_ready = signal("gexp_ready", ("G",))
        gmax_ready = signal("gmax_ready", ("G",))
        hw_ready = signal("hw_ready", ("G",))
        split_T1, split_T2 = signal("split_T1", ("T1",)), signal("split_T2", ("T2",))
        split_T3 = signal("split_T3", ("T3",))
        high_QK2 = signal("high_QK2", ("QK2",))
        neg_copied = signal("neg_copied", ("NT", "NT2"))
        mx2_ready = signal("mx2_ready", ("NT2",))
        res_ready = rd_sig["OP2"]
        rr_ready = signal("rr_ready", ("PS",))
        rinv_ready = signal("rinv_ready", ("PV",))
        sums2_ready = signal("sums2_ready", ("PV2",))
        rinv2_ready = signal("rinv2_ready", ("PV2",))
        norms = []
        for k, s, i in SCHED:
            norms += [(k, s, j) for j in range({"EMB": 3, "OP": 1}.get(k, 0))]
        var_ready, rstd_ready = ("var_ready", sem("var_ready")), ("rstd_ready", sem("rstd_ready"))
        steps["var_ready"] = steps["rstd_ready"] = norms
        x_loaded = [sem(f"x_loaded{s}") for s in range(2)]
        stored = [sem(f"stored{s}") for s in range(2)]
        consts_loaded = sem("consts_loaded")
        fills = sem("fills")
        setup_pe, setup_dve, setup_w = sem("setup_pe"), sem("setup_dve"), sem("setup_w")
        dve_chain, act_chain, pool_chain = sem("dve_chain"), sem("act_chain"), sem("pool_chain")

        def wait(eng, it, sig, p):
            n = steps[sig[0]]
            eng.wait_ge(sig[1], it * len(n) + n.index(p) + 1)

        def wait_earlier(eng, it, sig):
            eng.wait_ge(sig[1], it * len(steps[sig[0]]))

        loads = [(emb_raw, w_emb), (ln1_sb, ln1), (ln1b_raw, ln1_bias), (tokc, tok_const), (tok_b, tok_bias), (qk_raw, w_qk),
                 (v_raw, w_v), (out_w, w_out), (gl_w, w_gl), (qkv2_raw, w_qkv2), (lorab_raw, w_lora_b),
                 (bias2_raw, w_bias2), (proj_w, w_proj), (scale_sb, scale), (rowc, row_const),
                 (mats_sb, mats), (sel_raw, sel)]
        e_order = [p for p in SCHED if p[0] in ("ST", "ST2")]
        pv_order, pv2_order = steps["made_PV"], steps["made_PV2"]

        def wait_use(eng, it, kind, p):
            order = steps["made_" + kind]
            n = order.index(p)
            if n >= 2:
                wait(eng, it, rd_sig[kind], order[n - 2])
            else:
                wait_earlier(eng, it, rd_sig[kind])

        def wait_high(eng, it, s):
            if s == 0:
                wait(eng, it, qkn_ready, ("PS", 1, 0))
            else:
                wait(eng, it, rd_sig["QK2"], ("QK2", 0, 1))

        def tile_cols(t):
            return slice(TO * t, TO * t + TR)

        def key_rows(t):
            return TO if t == 0 else TR

        NFILLS = 20

        block = ctx.enter_context(nc.Block())

        @block.sync
        def _(sp):
            for dst, src in loads:
                sp.dma_start(dst[tuple(slice(None) for _ in src.shape)], src).then_inc(consts_loaded, 16)

            def load(it, s):
                sp.dma_start(xb[s][:], x_t[bass.ds(it * 2 + s, 1)].rearrange("b p c t -> (b p) c t")
                             ).then_inc(x_loaded[s], 16)

            def store(it, s):
                wait(sp, it, res_ready, ("OP2", s, 0))
                dst = out[bass.ds(it * 2 + s, 1)].rearrange("b t d -> (b t) d")
                sp.dma_start(dst[1:1 + TO], res[s][0:TO, 0, :]).then_inc(stored[s], 16)
                sp.dma_start(dst[1 + TO:NT], res[s][0:TO, 1, :]).then_inc(stored[s], 16)
                sp.dma_start(dst[0:1], res[s][TO:TR, 1, :]).then_inc(stored[s], 16)

            for s in range(2):
                load(0, s)
            with sp.Fori(0, ITERS - 1) as it:
                for s in range(2):
                    wait(sp, it, pe_sig["EMB"], ("EMB", s, 0))
                    wait(sp, it, xsq_ready, ("EMB", s, 0))
                    load(it + 1, s)
                for s in range(2):
                    store(it, s)
            for s in range(2):
                store(ITERS - 1, s)
            for s in range(2):
                sp.wait_ge(stored[s], 48 * ITERS)

        @block.gpsimd
        def _(pool):
            nc.gpsimd.memset(ones[:], 1.0).then_inc(fills, 1)
            nc.gpsimd.memset(emb_w[:, :, D:D + 1], 1.0).then_inc(fills, 1)
            for t in (high, low, *qa, *qb):
                nc.gpsimd.memset(t[:], 0.0).then_inc(fills, 1)
            for s in range(2):
                nc.gpsimd.memset(v2[s][:, :, :, DH2:2 * DH2], 1.0).then_inc(fills, 1)
                nc.gpsimd.memset(gates[s][:, :, NE:16], -1.0).then_inc(fills, 1)
                nc.gpsimd.memset(neg[s][:], 0.0).then_inc(fills, 1)
                nc.gpsimd.memset(comb[s][:, :, NE:NE + 1], 1.0).then_inc(fills, 1)
            nc.gpsimd.memset(half_neg[:], -0.5).then_inc(fills, 1)
            nc.gpsimd.memset(eps_ln[:], EPS).then_inc(fills, 1)
            nc.gpsimd.memset(tiny[:], 2.0 ** -62).then_inc(fills, 1)
            nc.gpsimd.memset(eps_qk[:], 1e-8).then_inc(fills, 1)
            pool.wait_ge(setup_dve, 2)
            for s in range(2):
                nc.gpsimd.memset(vx[s][:, :, :, DH:2 * DH], 1.0).then_inc(fills, 1)
            pool.wait_ge(fills, NFILLS + 2)
            with pool.Fori(0, ITERS) as it:
                for n, p in enumerate(norms):
                    wait(pool, it, var_ready, p)
                    nc.gpsimd.tensor_tensor(veps[:], mv[:, :, 1], eps_ln[:], ALU.add).then_inc(pool_chain, 1)
                    pool.wait_ge(pool_chain, it * len(norms) + n + 1)
                    nc.gpsimd.tensor_tensor(rstd[:], veps[:], half_neg[:], ALU.pow).then_inc(rstd_ready[1], 1)

        @block.tensor
        def _(pe):
            pe.wait_ge(consts_loaded, 16 * len(loads))
            pe.wait_ge(fills, NFILLS)
            pe.wait_ge(setup_dve, 1)
            for c in range(KC):
                nc.tensor.matmul(psum[0:TR, 0, 0:D], ones[:], emb_w[:, c, 0:D],
                                 start=(c == 0), stop=(c == KC - 1))
            for c in range(KC):
                mm = nc.tensor.matmul(psum[0:TR, 1, 0:D], ln1b_raw[:, c, :], emb_raw[:, c, :],
                                      start=(c == 0), stop=(c == KC - 1))
            mm.then_inc(setup_pe, 1)
            pe.wait_ge(setup_dve, 2)
            pe.wait_ge(fills, NFILLS + 2)
            SPLIT = ((0, 0), (0, 1), (1, 0))

            def ps(p, rows, cols, b=0):
                return psum[rows, bank[p] + b, cols]

            def transposes(p, src, width):
                for t in range(2):
                    n = key_rows(t)
                    last_mm = nc.tensor.transpose(ps(p, slice(0, width), slice(TO * t, TO * t + n)),
                                                  src(t, n), ident[0:n, 0:n])
                return last_mm

            def hidden_transposed(p, src):
                for c in range(2):
                    for t in range(2):
                        n = key_rows(t)
                        at = NT * c + TO * t
                        mm = nc.tensor.transpose(ps(p, slice(0, HC), slice(at, at + n)),
                                                 src[0:n, t, HC * c:HC * c + HC], ident[0:n, 0:n])
                return mm

            with pe.Fori(0, ITERS) as it:
                for p in SCHED:
                    kind, s, i = p
                    if before[p]:
                        wait(pe, it, rd_sig[before[p][0]], before[p])
                    else:
                        wait_earlier(pe, it, rd_sig[last[bank[p]][0]])
                    if kind == "EMB":
                        pe.wait_ge(x_loaded[s], it * 16 + 16)
                        for t in range(2):
                            for c in range(KC):
                                nc.tensor.matmul(ps(p, slice(0, TR), slice(194 * t, 194 * t + D + 1)),
                                                 xb[s][:, c, tile_cols(t)], emb_w[:, c, :],
                                                 start=(c == 0), stop=(c == KC - 1))
                        wait(pe, it, xss_ready, p)
                        for t in range(2):
                            mm = nc.tensor.matmul(ps(p, slice(0, TR), slice(194 * t + 193, 194 * t + 194)),
                                                  xss[s][:, tile_cols(t)], ones[:, 0:1],
                                                  start=True, stop=True)
                    elif kind == "T1":
                        wait(pe, it, hn_ready, ("EMB", s, 0))
                        mm = hidden_transposed(p, hn[s])
                    elif kind == "QK":
                        wait(pe, it, rd_sig["T1"], ("T1", s, 0))
                        for m in range(4):
                            f = 128 * (4 * i + m)
                            at = NT * (m % 2)
                            for n, (c, w, v) in enumerate((c, *wv) for c in range(2) for wv in SPLIT):
                                mm = nc.tensor.matmul(ps(p, slice(0, 128), slice(at, at + NT), m // 2),
                                                      qk_w[:, w, c, f:f + 128], hn_s[s][:, v, c, 0:NT],
                                                      start=(n == 0), stop=(n == 5))
                    elif kind == "PS":
                        wait(pe, it, ss_ready, p)
                        mm = nc.tensor.matmul(ps(p, slice(0, 128), slice(0, 2 * NT)), pair_sum,
                                              ss[s][:].rearrange("p a t -> p (a t)"), start=True, stop=True)
                    elif kind == "V":
                        for b in range(2):
                            for n, (c, w, v) in enumerate((c, *wv) for c in range(2) for wv in SPLIT):
                                mm = nc.tensor.matmul(ps(p, slice(0, TR), slice(0, INNER // 2), b),
                                                      hn_s[s][:, v, c, tile_cols(i)],
                                                      v_w[:, w, c, INNER // 2 * b:INNER // 2 * (b + 1)],
                                                      start=(n == 0), stop=(n == 5))
                    elif kind in ("SM", "SM2"):
                        if kind == "SM":
                            wait(pe, it, qkn_ready, ("PS", s, 0))
                        else:
                            wait(pe, it, rd_sig["QK2"], ("QK2", s, 1))
                        for e in range(2):
                            h = 2 * i + e
                            for t in range(2):
                                mm = nc.tensor.matmul(ps(p, slice(0, TR), slice(NT * t, NT * t + NT), e),
                                                      qa[s][:, h if kind == "SM" else h // 4, tile_cols(t)],
                                                      ka[s][:, h, 0:NT], start=True, stop=True)
                    elif kind in ("NT", "NT2"):
                        wait(pe, it, mx_ready if kind == "NT" else mx2_ready, p)
                        mm = transposes(p, lambda t, n: neg[s][0:n, t], 128)
                    elif kind in ("ST", "ST2"):
                        nt = "NT" if kind == "ST" else "NT2"
                        wait(pe, it, rd_sig[nt], (nt, s, 0))
                        for e in range(2):
                            h = 2 * i + e
                            g = h if kind == "ST" else h // 4
                            for t in range(2):
                                o = ps(p, slice(0, TR), slice(NT * t, NT * t + NT), e)
                                nc.tensor.matmul(o, ka[s][:, h, tile_cols(t)], qa[s][:, g, 0:NT],
                                                 start=True, stop=False)
                                mm = nc.tensor.matmul(o, kb[s][:, h, tile_cols(t)], qb[s][:, g, 0:NT],
                                                      start=False, stop=True)
                    elif kind == "PV":
                        wait(pe, it, rd_sig["ST"], ("ST", s, i))
                        wait(pe, it, rd_sig["V"], ("V", s, 1))
                        eb = ebuf[e_order.index(("ST", s, i)) % EBUFS]
                        for e in range(2):
                            for t in range(2):
                                n = key_rows(t)
                                mm = nc.tensor.matmul(ps(p, slice(0, 128), slice(NT * e, NT * e + NT)),
                                                      vx[s][0:n, t, 2 * i + e, :], eb[0:n, e, t, :],
                                                      start=(t == 0), stop=(t == 1))
                    elif kind == "OP":
                        wait(pe, it, rd_sig["PV"], ("PV", s, 5))
                        for t in range(2):
                            for m in range(H // 2):
                                mm = nc.tensor.matmul(ps(p, slice(0, TR), slice(D * t, D * t + D)),
                                                      o_t[s][:, m, tile_cols(t)], out_w[:, m, :],
                                                      start=(m == 0), stop=(m == H // 2 - 1))
                    elif kind == "T2":
                        wait(pe, it, hn2_ready, ("OP", s, 0))
                        mm = hidden_transposed(p, hn[s])
                    elif kind == "G":
                        wait(pe, it, rd_sig["T2"], ("T2", s, 0))
                        for t in range(2):
                            for c in range(2):
                                mm = nc.tensor.matmul(ps(p, slice(0, TR), slice(136 * t, 136 * t + 136)),
                                                      hn2_t[s][:, c, tile_cols(t)], gl_w[:, c, :],
                                                      start=(c == 0), stop=(c == 1))
                    elif kind == "T3":
                        wait(pe, it, hw_ready, ("G", s, 0))
                        transposes(p, lambda t, n: hw[s][0:n, t].rearrange("p e r -> p (e r)"), 128)
                        for t in range(2):
                            n = key_rows(t)
                            mm = nc.tensor.transpose(
                                ps(p, slice(0, 3 * (NE + 1)), slice(NT + TO * t, NT + TO * t + n)),
                                comb3[s][0:n, t].rearrange("p a b -> p (a b)"), ident[0:n, 0:n])
                    elif kind == "QK2":
                        wait(pe, it, rd_sig["T3"], ("T3", s, 0))
                        for m in range(G2):
                            o = ps(p, slice(0, 128), slice(NT * (m % 2), NT * (m % 2) + NT), m // 2)
                            f = slice(128 * (G2 * i + m), 128 * (G2 * i + m) + 128)
                            for w, v in SPLIT:
                                for c in range(2):
                                    nc.tensor.matmul(o, qkv2_w[:, w, c, f], hn2_s[s][:, v, c, 0:NT],
                                                     start=(c + w + v == 0), stop=False)
                                nc.tensor.matmul(o, lorab_w[:, w, f], hw_s[s][:, v, 0:NT], start=False, stop=False)
                            mm = nc.tensor.matmul(o, bias2_w[:, f], comb_t[s][:, 0:NT], start=False, stop=True)
                    elif kind == "V2":
                        f = slice(QKV2 - D, QKV2)
                        for t in range(2):
                            o = ps(p, slice(0, TR), slice(D * t, D * t + D))
                            for w, v in SPLIT:
                                for c in range(2):
                                    nc.tensor.matmul(o, hn2_s[s][:, v, c, tile_cols(t)], qkv2_w[:, w, c, f],
                                                     start=(c + w + v == 0), stop=False)
                                nc.tensor.matmul(o, hw_s[s][:, v, tile_cols(t)], lorab_w[:, w, f],
                                                 start=False, stop=False)
                            mm = nc.tensor.matmul(o, comb_t[s][:, tile_cols(t)], bias2_w[:, f],
                                                  start=False, stop=True)
                    elif kind == "PV2":
                        wait(pe, it, rd_sig["ST2"], ("ST2", s, 2 * i + 1))
                        wait(pe, it, rd_sig["V2"], ("V2", s, 0))
                        for t in range(2):
                            n = key_rows(t)
                            for j in range(4):
                                eb = ebuf[e_order.index(("ST2", s, 2 * i + j // 2)) % EBUFS]
                                mm = nc.tensor.matmul(ps(p, slice(32 * j, 32 * j + 32), slice(0, NT)),
                                                      v2[s][0:n, t, 4 * i + j, :], eb[0:n, j % 2, t, :],
                                                      start=(t == 0), stop=(t == 1))
                    elif kind == "OP2":
                        wait(pe, it, rd_sig["PV2"], ("PV2", s, 2))
                        for t in range(2):
                            for m in range(3):
                                mm = nc.tensor.matmul(ps(p, slice(0, TR), slice(D * t, D * t + D)),
                                                      o2_t[s][:, m, tile_cols(t)], proj_w[:, m, :],
                                                      start=(m == 0), stop=(m == 2))
                    mm.then_inc(pe_sig[kind][1], 1)

        @block.scalar
        def _(act):
            act.wait_ge(consts_loaded, 16 * len(loads))
            act.wait_ge(fills, NFILLS)
            act.wait_ge(setup_dve, 2)
            nc.scalar.preload_act_table_set("natural_log_exp_and_others")
            count = [0]

            def link(ins):
                count[0] += 1
                ins.then_inc(act_chain, 1)
                act.wait_ge(act_chain, count[0])

            with act.Fori(0, ITERS) as it:
                act.sem_clear(act_chain)
                count[0] = 0
                for p in SCHED:
                    kind, s, i = p
                    done = rd_sig[kind][1] if kind in rd_sig else None
                    b = bank[p]
                    if kind == "EMB":
                        act.wait_ge(x_loaded[s], it * 16 + 16)
                        if s == 0:
                            wait_earlier(act, it, ss_ready)
                        else:
                            wait(act, it, xss_ready, ("EMB", 0, 0))
                        nc.scalar.activation(xsq, xb[s][:], ACT.Square).then_inc(xsq_ready[1], 1)
                    elif kind in ("T1", "T2"):
                        wait(act, it, pe_sig[kind], p)
                        src = psum[0:HC, b, 0:2 * NT].rearrange("p (c t) -> p c t", c=2)
                        dst = hn_s if kind == "T1" else hn2_s
                        if kind == "T2":
                            nc.scalar.copy(hn2_t[s], src)
                        sig = split_T1 if kind == "T1" else split_T2
                        nc.scalar.copy(dst[s][:, 0, :, 0:NT], src).then_inc(sig[1], 1)
                    elif kind == "QK":
                        wait(act, it, pe_sig[kind], p)
                        src = psum[:, b:b + 2, 0:2 * NT]
                        if i == 0:
                            if s == 0:
                                wait(act, it, xss_ready, ("EMB", 1, 0))
                            else:
                                wait(act, it, ss_ready, ("PS", 0, 0))
                        nc.scalar.activation(
                            qk_sq[:, 4 * i:4 * i + 4, :].rearrange("p (b m) t -> p b (m t)", b=2),
                            src, ACT.Square, scale=1 / WS)
                        nc.scalar.mul(qk[s][:, 4 * i:4 * i + 4, :].rearrange("p (b m) t -> p b (m t)", b=2),
                                      src, 1 / WS).then_inc(done, 1)
                    elif kind == "PS":
                        wait(act, it, pe_sig[kind], p)
                        n2 = nrm[s]
                        nc.scalar.activation(n2, psum[:, b, 0:2 * NT], ACT.Ln, bias=tiny[:]).then_inc(done, 1)
                        wait(act, it, rd_sig[kind], p)
                        link(nc.scalar.activation(n2, n2, ACT.Exp, scale=0.5))
                        link(nc.scalar.activation(n2, n2, ACT.Ln, bias=eps_qk[:]))
                        nc.scalar.activation(n2, n2, ACT.Exp, scale=-0.5).then_inc(rr_ready[1], 1)
                    elif kind == "V":
                        wait(act, it, pe_sig[kind], p)
                        nc.scalar.mul(
                            vx[s][:, i, :, 0:DH].rearrange("p (b h) d -> p b h d", b=2),
                            psum[0:TR, b:b + 2, 0:INNER // 2].rearrange("p b (h d) -> p b h d", d=DH),
                            1 / WS).then_inc(done, 1)
                    elif kind in ("NT", "NT2"):
                        wait(act, it, pe_sig[kind], p)
                        nc.scalar.copy(qb[s][64:128, 0, 0:NT], psum[64:128, b, 0:NT]).then_inc(neg_copied[1], 1)
                    elif kind in ("ST", "ST2"):
                        wait(act, it, pe_sig[kind], p)
                        n = e_order.index(p)
                        if n >= EBUFS:
                            k0, s0, i0 = e_order[n - EBUFS]
                            user = ("PV", s0, i0) if k0 == "ST" else ("PV2", s0, i0 // 2)
                            wait(act, it, pe_sig[user[0]], user)
                        else:
                            wait_earlier(act, it, pe_sig["PV2"])
                        nc.scalar.activation(ebuf[n % EBUFS][:].rearrange("p e a t -> p e (a t)"),
                                             psum[0:TR, b:b + 2, 0:2 * NT], ACT.Exp).then_inc(done, 1)
                    elif kind == "PV":
                        wait(act, it, pe_sig[kind], p)
                        wait_use(act, it, "PV", p)
                        r = rinv[pv_order.index(p) % 2][:]
                        link(nc.scalar.activation(r, psum[DH:128, b, 0:2 * NT], ACT.Ln))
                        nc.scalar.activation(r, r, ACT.Exp, scale=-1.0).then_inc(rinv_ready[1], 1)
                    elif kind == "PV2":
                        wait(act, it, sums2_ready, p)
                        r = sums2[pv2_order.index(p) % 2][:]
                        link(nc.scalar.activation(r, r, ACT.Ln))
                        nc.scalar.activation(r, r, ACT.Exp, scale=-1.0).then_inc(rinv2_ready[1], 1)
                    elif kind == "G":
                        wait(act, it, gmax_ready, p)
                        nc.scalar.activation(gates[s][:, :, 0:NE], gl[s][:, :, 0:NE], ACT.Exp
                                             ).then_inc(gexp_ready[1], 1)
                    elif kind == "T3":
                        wait(act, it, pe_sig[kind], p)
                        nc.scalar.copy(comb_t[s][:, 0:NT], psum[0:3 * (NE + 1), b, NT:2 * NT])
                        nc.scalar.copy(hw_s[s][:, 0, 0:NT], psum[:, b, 0:NT]).then_inc(split_T3[1], 1)
                    elif kind == "QK2":
                        wait(act, it, pe_sig[kind], p)
                        dst, f = (qa[s], QSCALE / WS) if i == 0 else (high, 1 / WS)
                        if i == 1:
                            wait_high(act, it, s)
                        nc.scalar.mul(dst[:, 0:2, 0:NT],
                                      psum[:, b, 0:2 * NT].rearrange("p (m t) -> p m t", m=2), f)
                        nc.scalar.mul(dst[:, 2, 0:NT], psum[:, b + 1, 0:NT], f).then_inc(high_QK2[1], 1)
                    elif kind == "V2":
                        wait(act, it, pe_sig[kind], p)
                        nc.scalar.mul(v2[s][:, :, :, 0:DH2],
                                      psum[0:TR, b, 0:2 * D].rearrange("p (a h d) -> p a h d", a=2, d=DH2),
                                      1 / WS).then_inc(done, 1)

        @block.vector
        def _(dve):
            count = [0]

            def link(ins):
                count[0] += 1
                ins.then_inc(dve_chain, 1)
                dve.wait_ge(dve_chain, count[0])

            dve.wait_ge(consts_loaded, 16 * len(loads))
            dve.wait_ge(fills, NFILLS)
            nc.vector.tensor_tensor(emb_w[:, :, 0:D], emb_raw,
                                    ln1_sb[:].unsqueeze(2).broadcast_to([128, KC, D]), ALU.mult
                                    ).then_inc(setup_dve, 1)
            nc.vector.reciprocal(inv_scale[:], scale_sb[:])
            for s in range(2):
                nc.vector.tensor_copy(kb[s][64:128], sel_raw[64:128].broadcast_to([64, H, NTP]))

            def split_weights(dst, raw):
                nc.vector.tensor_scalar(dst(0), raw, WS, None, ALU.mult).then_inc(setup_w, 1)
                splits[0] += 1
                dve.wait_ge(setup_w, splits[0])
                nc.vector.scalar_tensor_tensor(out=dst(1), in0=raw, scalar=WS, in1=dst(0),
                                               op0=ALU.mult, op1=ALU.subtract)

            splits = [0]
            split_weights(lambda v: qk_w[:, v], qk_raw)
            split_weights(lambda v: v_w[:, v], v_raw)
            split_weights(lambda v: qkv2_w[:, v], qkv2_raw)
            split_weights(lambda v: lorab_w[:, v], lorab_raw[:, 0])
            nc.vector.tensor_scalar(bias2_raw[:, 0], bias2_raw[:, 0], WS, None, ALU.mult).then_inc(setup_w, 1)
            dve.wait_ge(setup_w, 5)
            nc.vector.tensor_copy(bias2_w[:], bias2_raw[:, 0]).then_inc(setup_w, 1)
            dve.wait_ge(setup_w, 6)
            nc.vector.scalar_tensor_tensor(out=bias2_w[:], in0=bias2_w[:], scalar=low_row, in1=bias2_raw[:, 0],
                                           op0=ALU.mult, op1=ALU.add)
            dve.wait_ge(setup_pe, 1)
            nc.vector.tensor_copy(emb_cs[:], psum[0:TR, 0, 0:D])
            nc.vector.tensor_tensor(emb_b[:], tok_b[:, 0, :], psum[0:TR, 1, 0:D], ALU.add
                                    ).then_inc(setup_dve, 1)
            dve.wait_ge(setup_dve, 2)

            def inverse_std(p):
                wait(dve, it, rstd_ready, p)

            def layernorm(p, src, dst, sig=None):
                for t in range(2):
                    a = nc.vector.bn_stats(st6[:, t, :], src[:, t, :])
                link(a)
                for t in range(2):
                    a = nc.vector.bn_aggr(mv[:, t, :], st6[:, t, :])
                a.then_inc(var_ready[1], 1)
                inverse_std(p)
                for t in range(2):
                    a = nc.vector.tensor_scalar(dst[:, t, :], src[:, t, :], mv[:, t, 0:1], rstd[:, t:t + 1],
                                                ALU.subtract, ALU.mult)
                if sig is None:
                    link(a)
                else:
                    a.then_inc(sig[1], 1)

            with dve.Fori(0, ITERS) as it:
                dve.sem_clear(dve_chain)
                count[0] = 0
                for p in SCHED:
                    kind, s, i = p
                    done = rd_sig[kind][1] if kind in rd_sig else None
                    b = bank[p]
                    if kind == "EMB":
                        wait(dve, it, xsq_ready, p)
                        nc.vector.tensor_reduce(xss[s][:], xsq.rearrange("p c t -> p t c"), AX.X, ALU.add
                                                ).then_inc(xss_ready[1], 1)
                        wait(dve, it, pe_sig[kind], p)
                        sums = psum[0:TR, b, 0:388].rearrange("p (t f) -> p t f", t=2)
                        link(nc.vector.tensor_scalar(nmean[:], sums[:, :, D], -1.0 / PD, None, ALU.mult))
                        link(nc.vector.tensor_tensor(msq[:], nmean[:], nmean[:], ALU.mult))
                        nc.vector.scalar_tensor_tensor(out=mv[:, :, 1], in0=sums[:, :, D + 1], scalar=1.0 / PD,
                                                            in1=msq[:], op0=ALU.mult, op1=ALU.subtract
                                                            ).then_inc(var_ready[1], 1)
                        inverse_std(("EMB", s, 0))
                        for t in range(2):
                            a = nc.vector.scalar_tensor_tensor(out=lnt[:, t, :], in0=emb_cs[:],
                                                               scalar=nmean[:, t:t + 1], in1=sums[:, t, 0:D],
                                                               op0=ALU.mult, op1=ALU.add)
                        a.then_inc(done, 1)
                        wait(dve, it, rd_sig[kind], p)
                        for t in range(2):
                            a = nc.vector.scalar_tensor_tensor(out=lnt[:, t, :], in0=lnt[:, t, :],
                                                               scalar=rstd[:, t:t + 1], in1=emb_b[:],
                                                               op0=ALU.mult, op1=ALU.add)
                        link(a)
                        layernorm(("EMB", s, 1), lnt, h0[s])
                        link(nc.vector.tensor_tensor(h0[s][:], h0[s][:], tokc[:, 0], ALU.mult))
                        link(nc.vector.tensor_tensor(h0[s][:], h0[s][:], tokc[:, 1], ALU.add))
                        layernorm(("EMB", s, 2), h0[s], hn[s], hn_ready)
                        wait(dve, it, hn_ready, p)
                        link(nc.vector.tensor_tensor(h0[s][:], h0[s][:],
                                                     b_out.unsqueeze(1).broadcast_to([TR, 2, D]), ALU.add))
                    elif kind in ("T1", "T2"):
                        wait(dve, it, split_T1 if kind == "T1" else split_T2, p)
                        dst = (hn_s if kind == "T1" else hn2_s)[s]
                        nc.vector.tensor_tensor(dst[:, 1, :, 0:NT],
                                                psum[0:HC, b, 0:2 * NT].rearrange("p (c t) -> p c t", c=2),
                                                dst[:, 0, :, 0:NT], ALU.subtract).then_inc(done, 1)
                    elif kind == "PS":
                        wait(dve, it, rd_sig["QK"], ("QK", s, 2))
                        for a in range(2):
                            r = nc.vector.tensor_reduce(ss[s][:, a, :],
                                                        qk_sq[:, 6 * a:6 * a + 6, :].rearrange("p m t -> p t m"),
                                                        AX.X, ALU.add)
                        r.then_inc(ss_ready[1], 1)
                        wait(dve, it, rr_ready, p)
                        for m in range(6):
                            nc.vector.scalar_tensor_tensor(out=qk[s][:, m, :], in0=qk[s][:, m, :],
                                                           scalar=inv_scale[:, m:m + 1], in1=nrm[s][:, 0:NT],
                                                           op0=ALU.mult, op1=ALU.mult)
                        link(nc.vector.tensor_tensor(qk[s][:, 6:12, :], qk[s][:, 6:12, :],
                                                     nrm[s][:, NT:2 * NT].unsqueeze(1).broadcast_to([128, 6, NT]),
                                                     ALU.mult))
                        for first, spread in ((0, ((qa, 0, high), (qa, 64, low), (qb, 0, high))),
                                              (6, ((ka, 0, high), (ka, 64, high), (kb, 0, low)))):
                            src = qk[s][:, first:first + 6, :]
                            link(nc.vector.tensor_copy(high[:, :, 0:NT], src))
                            link(nc.vector.tensor_tensor(low[:, :, 0:NT], src, high[:, :, 0:NT], ALU.subtract))
                            for dst, r, part in spread:
                                for e in range(2):
                                    a = nc.vector.tensor_copy(
                                        dst[s][r:r + 64, :, :].rearrange("p (m e) t -> p m e t", e=2)[:, :, e, :],
                                        part[64 * e:64 * e + 64])
                            if first == 0:
                                link(a)
                        a.then_inc(qkn_ready[1], 1)
                    elif kind in ("SM", "SM2"):
                        wait(dve, it, pe_sig[kind], p)
                        nc.vector.tensor_reduce(
                            mx[s][:, :, 2 * i:2 * i + 2].rearrange("p a e -> p e a"),
                            psum[0:TR, b:b + 2, 0:2 * NT].rearrange("p e (a t) -> p e a t", a=2),
                            AX.X, ALU.max).then_inc(done, 1)
                        if i == 5:
                            wait(dve, it, rd_sig[kind], p)
                            ready = mx_ready if kind == "SM" else mx2_ready
                            nc.vector.tensor_scalar(neg[s][:, :, 64:64 + H], mx[s][:], -1.0, None, ALU.mult
                                                    ).then_inc(ready[1], 1)
                    elif kind in ("NT", "NT2"):
                        wait(dve, it, neg_copied, p)
                        n = (H if kind == "NT" else G2) - 1
                        nc.vector.tensor_copy(qb[s][64:128, 1:1 + n, :],
                                              qb[s][64:128, 0:1, :].broadcast_to([64, n, NTP])).then_inc(done, 1)
                    elif kind == "PV":
                        wait(dve, it, rinv_ready, p)
                        r = rinv[pv_order.index(p) % 2]
                        for e in range(2):
                            a = nc.vector.tensor_tensor(o_t[s][DH * e:DH * e + DH, i, :],
                                                        psum[0:DH, b, NT * e:NT * e + NT],
                                                        r[:, NT * e:NT * e + NT], ALU.mult)
                        a.then_inc(done, 1)
                    elif kind == "OP":
                        dve.wait_ge(stored[s], it * 48)
                        wait(dve, it, pe_sig[kind], p)
                        nc.vector.tensor_tensor(h1[s][:].rearrange("p a d -> p (a d)"), psum[0:TR, b, 0:2 * D],
                                                h0[s][:].rearrange("p a d -> p (a d)"), ALU.add).then_inc(done, 1)
                        wait(dve, it, rd_sig[kind], p)
                        layernorm(("OP", s, 0), h1[s], hn[s], hn2_ready)
                        wait(dve, it, hn2_ready, p)
                        link(nc.vector.tensor_tensor(h1[s][:], h1[s][:],
                                                     b_proj.unsqueeze(1).broadcast_to([TR, 2, D]), ALU.add))
                    elif kind == "G":
                        wait(dve, it, pe_sig[kind], p)
                        nc.vector.tensor_tensor(gl[s][:], psum[0:TR, b, 0:272].rearrange("p (t f) -> p t f", t=2),
                                                b_gl.unsqueeze(1).broadcast_to([TR, 2, 136]), ALU.add
                                                ).then_inc(done, 1)
                        wait(dve, it, rd_sig[kind], p)
                        link(nc.vector.tensor_reduce(gmax[:], gl[s][:, :, 0:NE], AX.X, ALU.max))
                        nc.vector.tensor_tensor(gl[s][:, :, 0:NE], gl[s][:, :, 0:NE],
                                                gmax[:].unsqueeze(2).broadcast_to([TR, 2, NE]), ALU.subtract
                                                ).then_inc(gmax_ready[1], 1)
                        wait(dve, it, gexp_ready, p)
                        link(nc.vector.tensor_reduce(gsum[:], gates[s][:, :, 0:NE], AX.X, ALU.add))
                        link(nc.vector.reciprocal(gsum[:], gsum[:]))
                        link(nc.vector.tensor_scalar(gsum[:], gsum[:], LORA_SCALE, None, ALU.mult))
                        for t in range(2):
                            a = nc.vector.max(top8[:, t, :], gates[s][:, t, :])
                        link(a)
                        link(nc.vector.memset(top8[:, :, 2:8], -1.0))
                        for t in range(2):
                            a = nc.vector.match_replace(rest[:, t, :], top8[:, t, :], gates[s][:, t, :], 0.0)
                        link(a)
                        link(nc.vector.tensor_tensor(rest[:, :, 0:NE], gates[s][:, :, 0:NE], rest[:, :, 0:NE],
                                                     ALU.subtract))
                        link(nc.vector.tensor_tensor(comb[s][:, :, 0:NE], rest[:, :, 0:NE],
                                                     gsum[:].unsqueeze(2).broadcast_to([TR, 2, NE]), ALU.mult))
                        nc.vector.tensor_copy(comb_h[:], comb[s][:])
                        for t in range(2):
                            a = nc.vector.tensor_tensor(
                                hw[s][:, t], gl[s][:, t, NE:].rearrange("p (e r) -> p e r", e=NE),
                                comb[s][:, t, 0:NE].unsqueeze(2).broadcast_to([TR, NE, RANK]), ALU.mult)
                        link(a)
                        for part in (0, 2):
                            nc.vector.tensor_copy(comb3[s][:, :, part, :], comb_h[:])
                        nc.vector.tensor_tensor(comb3[s][:, :, 1, :], comb[s][:], comb_h[:], ALU.subtract
                                                ).then_inc(hw_ready[1], 1)
                    elif kind == "T3":
                        wait(dve, it, split_T3, p)
                        nc.vector.tensor_tensor(hw_s[s][:, 1, 0:NT], psum[:, b, 0:NT], hw_s[s][:, 0, 0:NT],
                                                ALU.subtract).then_inc(done, 1)
                    elif kind == "QK2":
                        wait(dve, it, high_QK2, p)
                        pair = psum[:, b, 0:2 * NT].rearrange("p (m t) -> p m t", m=2)
                        if i == 0:
                            nc.vector.tensor_copy(qb[s][0:64, 0:G2, :], qa[s][0:64, 0:G2, :])
                            for dst, src in ((qa[s][64:128, 0:2, 0:NT], pair[64:128]),
                                             (qa[s][64:128, 2, 0:NT], psum[64:128, b + 1, 0:NT])):
                                a = nc.vector.scalar_tensor_tensor(out=dst, in0=src, scalar=QSCALE / WS, in1=dst,
                                                                   op0=ALU.mult, op1=ALU.subtract)
                        else:
                            for j, src in ((slice(0, 2), pair[0:64]), (2, psum[0:64, b + 1, 0:NT])):
                                a = nc.vector.scalar_tensor_tensor(out=low[0:64, j, 0:NT], in0=src, scalar=1 / WS,
                                                                   in1=high[0:64, j, 0:NT],
                                                                   op0=ALU.mult, op1=ALU.subtract)
                            link(a)
                            for j in range(4):
                                for dst, src in ((ka[s][:], high[:, 0:G2, :]), (kb[s][0:64], low[0:64, 0:G2, :])):
                                    n = src.shape[0]
                                    a = nc.vector.tensor_scalar(
                                        dst.rearrange("p (g j) t -> p g j t", j=4)[:, :, j, :], src,
                                        masks[0:n, j:j + 1], None, ALU.mult)
                        a.then_inc(done, 1)
                    elif kind == "PV2":
                        wait(dve, it, pe_sig[kind], p)
                        o = o2_t[s][:, i, :]
                        link(nc.vector.tensor_copy(o, psum[:, b, 0:NT]))
                        r = sums2[pv2_order.index(p) % 2]
                        nc.vector.stream_shuffle(r[:], o, [j + 16 if j < 16 else j for j in range(32)]
                                                 ).then_inc(sums2_ready[1], 1)
                        wait(dve, it, rinv2_ready, p)
                        nc.vector.tensor_tensor(o, o, r[:], ALU.mult).then_inc(done, 1)
                    elif kind == "OP2":
                        wait(dve, it, pe_sig[kind], p)
                        nc.vector.tensor_tensor(res[s][:].rearrange("p a d -> p (a d)"), psum[0:TR, b, 0:2 * D],
                                                h1[s][:].rearrange("p a d -> p (a d)"), ALU.add
                                                ).then_inc(done, 1)


def kernel(x, L0_tok_ln1_g, L0_tok_ln1_b, L0_tok_W, L0_tok_b, L0_tok_ln2_g, L0_tok_ln2_b, L0_tok_cls,
           L0_attn_w_qkv, L0_attn_w_out, L0_attn_b_out, L0_attn_scale, L0_ffn_Wg, L0_ffn_bg, L0_ffn_Wqkv,
           L0_ffn_bqkv, L0_ffn_Wproj, L0_ffn_bproj, L0_ffn_A, L0_ffn_ba, L0_ffn_Bm, L0_ffn_bb):
    import concourse.bacc as bacc
    from concourse.bass_utils import run_bass_kernel_spmd

    f = np.float32
    p = np.asarray(x).reshape(B, 3, 14, 16, 14, 16).transpose(0, 3, 5, 1, 2, 4).reshape(B, KC, 128, NP)
    x_t = np.zeros((B, 128, KC, NT), f)
    x_t[..., :NP] = p.transpose(0, 2, 1, 3)

    def chunks(a, rows):
        a = np.asarray(a)
        return a.reshape(-1, rows, a.shape[-1]).transpose(1, 0, 2)

    ln1 = chunks(np.asarray(L0_tok_ln1_g).reshape(PD, 1), 128)[:, :, 0]
    ln1_bias = np.repeat(chunks(np.asarray(L0_tok_ln1_b).reshape(PD, 1), 128), TR, axis=2)
    tok_const = np.zeros((TR, 2, 2, D), f)
    tok_const[:, 0], tok_const[:, 1] = L0_tok_ln2_g, L0_tok_ln2_b
    tok_const[TR - 1, 0, 1] = 0
    tok_const[TR - 1, 1, 1] = np.asarray(L0_tok_cls)[0, 0]
    w_t = np.asarray(L0_attn_w_qkv).T
    w2 = np.asarray(L0_ffn_Wqkv).T
    twice = np.repeat(np.arange(2 * D).reshape(2 * G2, 1, 64), 2, axis=1).reshape(-1)
    order = np.r_[twice, 2 * D:3 * D]
    w_gl = np.concatenate([np.asarray(L0_ffn_Wg), np.asarray(L0_ffn_A).reshape(NE * RANK, D)]).T
    w_lora_b = np.asarray(L0_ffn_Bm).transpose(0, 2, 1).reshape(NE * RANK, 1, 3 * D)[:, :, order]
    w_bias2 = np.concatenate([np.asarray(L0_ffn_bb), np.asarray(L0_ffn_bqkv)[None]])[:, None, order]
    w_bias2 = np.concatenate([w_bias2] * 3)
    w_proj = np.zeros((3, 4, 32, D), f)
    w_proj[:, :, :DH2] = np.asarray(L0_ffn_Wproj).T.reshape(3, 4, DH2, D)
    scale = np.repeat(np.asarray(L0_attn_scale).reshape(H // 2, 2), DH, axis=1).T
    row = np.concatenate([np.asarray(L0_attn_b_out), np.asarray(L0_ffn_bproj), np.asarray(L0_ffn_bg),
                          np.asarray(L0_ffn_ba).reshape(-1)])
    row_const = np.repeat(row[None], TR, axis=0)
    mats = np.zeros((128, 261), f)
    r = np.arange(128)
    mats[r, r] = 1
    mats[:, 128:256] = (r[:, None] % DH == r[None, :] % DH)
    mats[r, 256 + r % 64 // DH2] = 1
    mats[2 * (NE + 1):3 * (NE + 1), 260] = -1
    sel = np.zeros((128, H, 1), f)
    sel[64 + np.arange(H), np.arange(H)] = 1

    arrays = {
        "x_t": x_t, "w_emb": chunks(L0_tok_W, 128), "ln1": ln1, "ln1_bias": ln1_bias, "tok_const": tok_const,
        "tok_bias": np.repeat(np.asarray(L0_tok_b)[None, None], TR, axis=0),
        "w_qk": chunks(w_t[:, :2 * INNER], HC), "w_v": chunks(w_t[:, 2 * INNER:], HC),
        "w_out": chunks(np.asarray(L0_attn_w_out).T, 128), "w_gl": chunks(w_gl, HC),
        "w_qkv2": chunks(w2[:, order], HC), "w_lora_b": w_lora_b, "w_bias2": w_bias2,
        "w_proj": chunks(w_proj.reshape(384, D), 128), "scale": scale, "row_const": row_const,
        "mats": mats, "sel": sel,
    }
    arrays = {k: np.ascontiguousarray(v) for k, v in arrays.items()}
    nc = bacc.Bacc("TRN2", target_bir_lowering=False, num_devices=1)
    args = [nc.dram_tensor(k, v.shape, mybir.dt.from_np(v.dtype), kind="ExternalInput").ap()
            for k, v in arrays.items()]
    out = nc.dram_tensor("out", (B, NT, D), mybir.dt.float32, kind="ExternalOutput").ap()
    vit_tower(nc, *args, out)
    return run_bass_kernel_spmd(nc, [arrays], core_ids=[0]).results[0]["out"]
```

```python
import numpy as np
import concourse.bass as bass
from concourse import mybir
from contextlib import ExitStack

B, D, NP = 64, 192, 196
NT = NP + 1
PD, KC = 768, 6
TR, TO = 99, 98
H, DH = 12, 64
DH2 = D // H
INNER = H * DH
NE, RANK = 8, 16
HC = D // 2
ITERS = B // 2
EPS = 1e-5
LORA_SCALE = 32 / RANK
NTP = NT + 1
G2 = 3
QKV2 = 2 * G2 * 128 + D
WS = 64.0
QSCALE = DH2 ** -0.5

ORDER = """
-X -OP@2 QK.0@4 -LD -T2@3 QK.1@0 -G@7 QK.2@4 -GB S -EMB@7 -T3@2 PS@6 N.0 -QK2.0@6 N.1 -QK2.1@0
N.2 -V2@2 -SM2.0@4 -SM2.1@2 N.3 -SM2.2@0 V.0@4 -SM2.3@2 -SM2.4@0 -SM2.5@6 V.1@4 SM.0@0 -NT2@7
SM.1@2 SM.2@4 -ST2.0@0 SM.3@6 -ST2.1@2 SM.4@0 SM.5@4 -ST2.2@6 -PV2.0@3 -M2.0 NT@0 -ST2.3@6
-ST2.4@2 -ST2.5@4 -PV2.1@6 ST.0@0 -PV2.2@4 ST.1@2 -LA ST.2@6 PV.0@4 M.0 PV.1@5 ST.3@0 -M2.1
ST.4@2 PV.2@6 -LB M.1 -M2.2 ST.5@0 PV.3@2 M.2 M.3 PV.4@3 PV.5@6 M.4 -LC M.5 -OP2@1 -T1@3
"""


def half_pass(s):
    for name in ORDER.split():
        step, _, b = name.lstrip("-").partition("@")
        kind, _, i = step.partition(".")
        yield (kind, 1 - s if name[0] == "-" else s, int(i or 0)), int(b) if b else None


BANK = dict([*half_pass(0), *half_pass(1)])
SCHED = list(BANK)
POS = {p: n for n, p in enumerate(SCHED)}
PRODUCTS = ("EMB", "T1", "QK", "PS", "V", "SM", "NT", "ST", "PV", "OP", "T2", "G", "T3", "QK2", "V2",
            "SM2", "NT2", "ST2", "PV2", "OP2")
EMBEDDING = ("X", "EMB", "LA", "LB", "LC", "T1")
BEHIND = {p for p in SCHED[:len(SCHED) // 2] if p[1] == 1 and p[0] not in EMBEDDING}
AHEAD = {p for p in SCHED if p[1] == 0 and p[0] in EMBEDDING}
WIDE = ("QK", "V", "SM", "ST", "QK2", "SM2", "ST2")
EBUFS = 4


def banks(p):
    return range(BANK[p], BANK[p] + (2 if p[0] in WIDE else 1))


class Pass:

    def __init__(self, which, it):
        self.which, self.it, self.at = which, it, None

    def does(self, p, which=None):
        return {"start": p in AHEAD, "first": p not in BEHIND, "middle": True, "final": p not in AHEAD,
                "last": p in BEHIND}[which or self.which]

    def did(self, p):
        before = {"start": None, "first": "start", "middle": "middle", "final": "middle", "last": "final"}
        return before[self.which] is not None and self.does(p, before[self.which])

    def steps(self):
        for p in SCHED:
            if self.does(p):
                self.at = p
                yield p

    def before(self, order):
        ahead, behind = len([q for q in order if q in AHEAD]), len([q for q in order if q in BEHIND])
        if self.which in ("start", "first"):
            return 0 if self.which == "start" else ahead
        if self.which == "last":
            ahead = 0
        return self.it * len(order) - behind + ahead

    def count(self, order, p, earlier=None):
        if earlier is None:
            earlier = POS[p] > POS[self.at] or not self.does(p)
        if not earlier:
            return self.before(order) + len([q for q in order if POS[q] <= POS[p] and self.does(q)])
        if not self.did(p):
            return None
        return self.before(order) - len([q for q in order if POS[q] > POS[p] and self.did(q)])

    def previous(self, users, p):
        for q in users[:users.index(p)][::-1]:
            if self.does(q):
                return q, False
        return next((q for q in users[::-1] if self.did(q)), users[-1]), True


def vit_tower(nc, x_t, w_emb, ln1, ln1_bias, tok_const, tok_bias, w_qk, w_v, w_out, w_gl, w_qkv2, w_lora_b,
              w_bias2, w_proj, scale, row_const, mats, sel, out):
    F32, F16 = mybir.dt.float32, mybir.dt.float16
    ALU, ACT, AX = mybir.AluOpType, mybir.ActivationFunctionType, mybir.AxisListType
    ctx = ExitStack()
    with ctx:
        def sb(name, shape, dt=F32):
            return ctx.enter_context(nc.sbuf_tensor(name, shape, dt))

        def two(name, shape, dt=F32):
            return [sb(f"{name}{s}", shape, dt) for s in range(2)]

        def sem(name):
            return ctx.enter_context(nc.semaphore(name))

        emb_w = sb("emb_w", [128, KC, D + 1])
        ln1_sb = sb("ln1_sb", [128, KC])
        tokc = sb("tokc", [TR, 2, 2, D])
        emb_cs = sb("emb_cs", [TR, D])
        emb_b = sb("emb_b", [TR, D])
        qk_w = sb("qk_w", [HC, 2, 2, 2 * INNER], F16)
        v_w = sb("v_w", [HC, 2, 2, INNER], F16)
        out_w = sb("out_w", [128, H // 2, D])
        gl_w = sb("gl_w", [HC, 2, NE + NE * RANK])
        qkv2_w = sb("qkv2_w", [HC, 2, 2, QKV2], F16)
        lorab_w = sb("lorab_w", [128, 2, QKV2], F16)
        bias2_w = sb("bias2_w", [3 * (NE + 1), QKV2], F16)
        proj_w = sb("proj_w", [128, 3, D])
        scale_sb = sb("scale_sb", [128, H // 2])
        inv_scale = sb("inv_scale", [128, H // 2])
        rowc = sb("rowc", [TR, 2 * D + NE + NE * RANK])
        mats_sb = sb("mats_sb", [128, 261])
        ident, pair_sum = mats_sb[:, 0:128], mats_sb[:, 128:256]
        masks = mats_sb[:, 256:260]
        low_row = mats_sb[0:3 * (NE + 1), 260:261]
        one_col = emb_w[:, 0, D:D + 1]
        b_out, b_proj = rowc[:, 0:D], rowc[:, D:2 * D]
        b_gl = rowc[:, 2 * D:]

        xb = two("xb", [128, KC, NT])
        xss = two("xss", [128, NT])
        h0, h1 = two("h0", [TR, 2, D]), two("h1", [TR, 2, D])
        hn = two("hn", [TR, 2, D])
        hn_s, hn2_s = two("hn_s", [HC, 2, 2, NTP], F16), two("hn2_s", [HC, 2, 2, NTP], F16)
        qk = two("qk", [128, H, NT])
        qk_sq = sb("qk_sq", [128, H, NT])
        xsq = qk_sq[:, 0:KC, :]
        qa, qb = two("qa", [128, H, NTP], F16), two("qb", [128, H, NTP], F16)
        ka, kb = two("ka", [128, H, NTP], F16), two("kb", [128, H, NTP], F16)
        high, low = sb("high", [128, H // 2, NTP], F16), sb("low", [128, H // 2, NTP], F16)
        ss = two("ss", [128, 2, NT])
        nrm = [ss[s][:].rearrange("p a t -> p (a t)") for s in range(2)]
        hn2_t = [ss[s][0:HC] for s in range(2)]
        vx = two("vx", [TR, 2, H, 2 * DH])
        mx = two("mx", [TR, 2, H])
        neg = two("neg", [TR, 2, 128])
        ebuf = [sb(f"ebuf{i}", [TR, 2, 2, NT]) for i in range(EBUFS)]
        rinv = two("rinv", [DH, 2 * NT])
        half_neg, eps_ln = sb("half_neg", [TR, 2]), sb("eps_ln", [TR, 2])
        tiny, eps_qk = sb("tiny", [128, 1]), sb("eps_qk", [128, 1])
        o_t = [qk[s][:, 0:H // 2, :] for s in range(2)]
        gl = two("gl", [TR, 2, NE + NE * RANK])
        gmax = sb("gmax", [TR, 2])
        gates = two("gates", [TR, 2, 16])
        top8 = sb("top8", [TR, 2, 8])
        rest = sb("rest", [TR, 2, 16])
        gsum = sb("gsum", [TR, 2])
        comb = two("comb", [TR, 2, NE + 1])
        high2, low2 = sb("high2", [128, G2, NTP], F16), sb("low2", [64, G2, NTP], F16)
        comb_h = sb("comb_h", [TR, 2, NE + 1], F16)
        comb3 = two("comb3", [TR, 2, 3, NE + 1])
        hw = [gl[s][:, :, NE:] for s in range(2)]
        hw_s = two("hw_s", [128, 2, NTP], F16)
        comb_t = two("comb_t", [3 * (NE + 1), NTP], F16)
        v2 = two("v2", [TR, 2, H, 2 * DH2])
        sums2 = two("sums2", [128, NT])
        o2_t = [qk[s][:, 6:9, :] for s in range(2)]
        res = h1
        st6 = two("st6", [TR, 2, 6])
        mv = two("mv", [TR, 2, 2])
        rstd = two("rstd", [TR, 2])
        veps = two("veps", [TR, 2])
        lnt = hn
        nmean = two("nmean", [TR, 2])
        msq = sb("msq", [TR, 2])

        def flat(t, rows, first, *shape):
            n = int(np.prod(shape))
            names = "abc"[:len(shape)]
            return t[0:rows].rearrange("p a t -> p (a t)")[:, first:first + n].rearrange(
                f"p ({' '.join(names)}) -> p {' '.join(names)}", **dict(zip(names, shape)))

        emb_raw = flat(qk_sq, 128, 0, KC, D)
        ln1b_raw = flat(qk_sq, 128, KC * D, KC, TR)
        tok_b = flat(qk_sq, TR, KC * (D + TR) + H, 1, D)
        sel_raw = flat(qk_sq, 128, KC * (D + TR), H, 1)
        vx_flat = [vx[s][:].rearrange("p a h d -> p (a h) d") for s in range(2)]
        qk_raw = flat(vx_flat[0], HC, 0, 2, 2 * INNER)
        v_raw = flat(vx_flat[1], HC, 0, 2, INNER)
        qkv2_raw = flat(qk[0], HC, 0, 2, QKV2)
        lorab_raw = flat(qk[1], 128, 0, 1, QKV2)
        bias2_raw = flat(qk[1], 3 * (NE + 1), QKV2, 1, QKV2)
        ones = flat(qk[1], 128, 2 * QKV2, 1, TR)[:, 0]

        psum = ctx.enter_context(nc.psum_tensor("psum", [128, 8, 512], F32))
        users = [[p for p in SCHED if p[0] in PRODUCTS and b in banks(p)] for b in range(8)]

        steps = {}

        def signal(name, kinds, only=lambda p: True):
            steps[name] = [p for p in SCHED if p[0] in kinds and only(p)]
            return name, sem(name)

        pe_sig = {k: signal("made_" + k, (k,)) for k in PRODUCTS}
        rd_sig = {k: signal("read_" + k, ("M",) if k == "PV" else (k,)) for k in PRODUCTS}
        hn_ready = signal("hn_ready", ("LC",))
        xss_ready = signal("xss_ready", ("X",))
        xsq_ready = signal("xsq_ready", ("X",))
        ss_ready = signal("ss_ready", ("S",))
        qkn_ready = signal("qkn_ready", ("N",))
        high_N = signal("high_N", ("N",), lambda p: p[2] % 2 == 1)
        spread = {(s, i): signal(f"spread_{'qk'[i // 2]}{s}", ("N",), lambda p, q=("N", s, i): p == q)
                  for s in range(2) for i in (1, 3)}
        h0_ready, h1_ready = signal("h0_ready", ("LC",)), signal("h1_ready", ("LD",))
        ka2_ready = signal("ka2_ready", ("QK2",), lambda p: p[2] == 1)
        o2_ready = signal("o2_ready", ("M2",))
        mx_ready = signal("mx_ready", ("NT",))
        hn2_ready = signal("hn2_ready", ("LD",))
        gexp_ready = signal("gexp_ready", ("G",))
        gmax_ready = signal("gmax_ready", ("G",))
        hw_ready = signal("hw_ready", ("GB",))
        split_T1, split_T2 = signal("split_T1", ("T1",)), signal("split_T2", ("T2",))
        split_T3 = signal("split_T3", ("T3",))
        high_QK2 = signal("high_QK2", ("QK2",))
        neg_copied = signal("neg_copied", ("NT", "NT2"))
        mx2_ready = signal("mx2_ready", ("NT2",))
        res_ready = rd_sig["OP2"]
        rr_ready = signal("rr_ready", ("PS",))
        rinv_ready = signal("rinv_ready", ("PV",))
        sums2_ready = rd_sig["PV2"]
        rinv2_ready = signal("rinv2_ready", ("PV2",))
        norm_steps = ("EMB", "LA", "LB", "OP")
        var_ready, rstd_ready = signal("var_ready", norm_steps), signal("rstd_ready", norm_steps)
        veps_made = signal("veps_made", norm_steps)
        x_loaded = [sem(f"x_loaded{s}") for s in range(2)]
        stored = [sem(f"stored{s}") for s in range(2)]
        consts_loaded = sem("consts_loaded")
        fills = sem("fills")
        setup_pe, setup_dve, setup_w = sem("setup_pe"), sem("setup_dve"), sem("setup_w")
        dve_chain, act_chain = sem("dve_chain"), sem("act_chain")

        def wait(eng, now, sig, p, earlier=None, by=1):
            n = now.count(steps[sig[0]], p, earlier)
            if n is not None:
                eng.wait_ge(sig[1], n * by)

        def reader(p):
            return rd_sig[p[0]], (("M", *p[1:]) if p[0] == "PV" else p)

        def wait_free(eng, now, order, freed):
            q, earlier = now.previous(order, now.at)
            wait(eng, now, *freed(q), earlier)

        def passes(eng, body):
            body(Pass("start", -1))
            body(Pass("first", 0))
            with eng.Fori(1, ITERS - 1) as it:
                body(Pass("middle", it))
            body(Pass("final", ITERS - 1))
            body(Pass("last", ITERS))

        loads = [(emb_raw, w_emb), (ln1_sb, ln1), (ln1b_raw, ln1_bias), (tokc, tok_const), (tok_b, tok_bias), (qk_raw, w_qk),
                 (v_raw, w_v), (out_w, w_out), (gl_w, w_gl), (qkv2_raw, w_qkv2), (lorab_raw, w_lora_b),
                 (bias2_raw, w_bias2), (proj_w, w_proj), (scale_sb, scale), (rowc, row_const),
                 (mats_sb, mats), (sel_raw, sel)]
        e_order = [p for p in SCHED if p[0] in ("ST", "ST2")]
        pv_order, pv2_order = steps["made_PV"], steps["made_PV2"]
        sq_users = [p for p in SCHED if p[0] == "X" or p[0] == "QK" and p[2] == 0]
        e_users = [e_order[n::EBUFS] for n in range(EBUFS)]
        rinv_users = [pv_order[n::2] for n in range(2)]
        split_users = steps["high_N"]
        high2_users = [p for p in SCHED if p[0] == "QK2" and p[2] == 1]

        def squares_used(p):
            return (xss_ready, p) if p[0] == "X" else (ss_ready, ("S", p[1], 0))

        def exp_used(p):
            q = ("PV", p[1], p[2]) if p[0] == "ST" else ("PV2", p[1], p[2] // 2)
            return pe_sig[q[0]], q

        def tile_cols(t):
            return slice(TO * t, TO * t + TR)

        def key_rows(t):
            return TO if t == 0 else TR

        NFILLS = 22

        block = ctx.enter_context(nc.Block())

        @block.sync
        def _(sp):
            for dst, src in loads:
                sp.dma_start(dst[tuple(slice(None) for _ in src.shape)], src).then_inc(consts_loaded, 16)

            def load(n, s):
                sp.dma_start(xb[s][:], x_t[bass.ds(n * 2 + s, 1)].rearrange("b p c t -> (b p) c t")
                             ).then_inc(x_loaded[s], 16)

            def body(now):
                for kind, s, i in now.steps():
                    if kind == "N" and i % 2 == 1:
                        wait(sp, now, qkn_ready, ("N", s, i))
                        for dst, r, part in (((qa, 0, high), (qa, 64, low), (qb, 0, high)) if i == 1 else
                                             ((ka, 0, high), (ka, 64, high), (kb, 0, low))):
                            for e in range(2):
                                sp.dma_start(dst[s][r:r + 64, 6 * e:6 * e + 6, :], part[64 * e:64 * e + 64]
                                             ).then_inc(spread[s, i][1], 16)
                    elif kind == "QK" and i == 0 and now.which in ("first", "middle"):
                        wait(sp, now, pe_sig["EMB"], ("EMB", s, 0))
                        wait(sp, now, xsq_ready, ("X", s, 0))
                        load(now.it + 1, s)
                    elif kind == "OP2":
                        wait(sp, now, res_ready, ("OP2", s, 0))
                        dst = out[bass.ds((now.it - s) * 2 + s, 1)].rearrange("b t d -> (b t) d")
                        sp.dma_start(dst[1:1 + TO], res[s][0:TO, 0, :]).then_inc(stored[s], 16)
                        sp.dma_start(dst[1 + TO:NT], res[s][0:TO, 1, :]).then_inc(stored[s], 16)
                        sp.dma_start(dst[0:1], res[s][TO:TR, 1, :]).then_inc(stored[s], 16)

            for s in range(2):
                load(0, s)
            passes(sp, body)
            for s in range(2):
                sp.wait_ge(stored[s], 48 * (ITERS + s))

        @block.gpsimd
        def _(pool):
            nc.gpsimd.memset(ones, 1.0).then_inc(fills, 1)
            nc.gpsimd.memset(emb_w[:, :, D:D + 1], 1.0).then_inc(fills, 1)
            for t in (high, low, high2, low2, *qa, *qb):
                nc.gpsimd.memset(t[:], 0.0).then_inc(fills, 1)
            for s in range(2):
                nc.gpsimd.memset(v2[s][:, :, :, DH2:2 * DH2], 1.0).then_inc(fills, 1)
                nc.gpsimd.memset(gates[s][:, :, NE:16], -1.0).then_inc(fills, 1)
                nc.gpsimd.memset(neg[s][:], 0.0).then_inc(fills, 1)
                nc.gpsimd.memset(comb[s][:, :, NE:NE + 1], 1.0).then_inc(fills, 1)
            nc.gpsimd.memset(rinv[1][:], 0.0).then_inc(stored[1], 48)
            nc.gpsimd.memset(half_neg[:], -0.5).then_inc(fills, 1)
            nc.gpsimd.memset(eps_ln[:], EPS).then_inc(fills, 1)
            nc.gpsimd.memset(tiny[:], 2.0 ** -62).then_inc(fills, 1)
            nc.gpsimd.memset(eps_qk[:], 1e-8).then_inc(fills, 1)
            pool.wait_ge(setup_dve, 2)
            for s in range(2):
                nc.gpsimd.memset(vx[s][:, :, :, DH:2 * DH], 1.0).then_inc(fills, 1)
            pool.wait_ge(fills, NFILLS + 2)

            def body(now):
                for p in now.steps():
                    s = p[1]
                    if p[0] == "LC":
                        wait(pool, now, hn_ready, p)
                        nc.gpsimd.tensor_tensor(h0[s][:], h0[s][:], b_out.unsqueeze(1).broadcast_to([TR, 2, D]),
                                                ALU.add).then_inc(h0_ready[1], 1)
                    elif p[0] == "LD":
                        wait(pool, now, hn2_ready, p)
                        nc.gpsimd.tensor_tensor(h1[s][:], h1[s][:], b_proj.unsqueeze(1).broadcast_to([TR, 2, D]),
                                                ALU.add).then_inc(h1_ready[1], 1)
                    elif p[0] in norm_steps:
                        wait(pool, now, var_ready, p)
                        nc.gpsimd.tensor_tensor(veps[s][:], mv[s][:, :, 1], eps_ln[:], ALU.add
                                                ).then_inc(veps_made[1], 1)
                        wait(pool, now, veps_made, p)
                        nc.gpsimd.tensor_tensor(rstd[s][:], veps[s][:], half_neg[:], ALU.pow
                                                ).then_inc(rstd_ready[1], 1)

            passes(pool, body)

        @block.tensor
        def _(pe):
            pe.wait_ge(consts_loaded, 16 * len(loads))
            pe.wait_ge(fills, NFILLS)
            pe.wait_ge(setup_dve, 1)
            for c in range(KC):
                nc.tensor.matmul(psum[0:TR, 0, 0:D], ones, emb_w[:, c, 0:D],
                                 start=(c == 0), stop=(c == KC - 1))
            for c in range(KC):
                mm = nc.tensor.matmul(psum[0:TR, 1, 0:D], ln1b_raw[:, c, :], emb_raw[:, c, :],
                                      start=(c == 0), stop=(c == KC - 1))
            mm.then_inc(setup_pe, 1)
            pe.wait_ge(setup_dve, 2)
            pe.wait_ge(fills, NFILLS + 2)
            SPLIT = ((0, 0), (0, 1), (1, 0))

            def ps(p, rows, cols, b=0):
                return psum[rows, BANK[p] + b, cols]

            def transposes(p, src, width):
                for t in range(2):
                    n = key_rows(t)
                    last_mm = nc.tensor.transpose(ps(p, slice(0, width), slice(TO * t, TO * t + n)),
                                                  src(t, n), ident[0:n, 0:n])
                return last_mm

            def hidden_transposed(p, src):
                for c in range(2):
                    for t in range(2):
                        n = key_rows(t)
                        at = NT * c + TO * t
                        mm = nc.tensor.transpose(ps(p, slice(0, HC), slice(at, at + n)),
                                                 src[0:n, t, HC * c:HC * c + HC], ident[0:n, 0:n])
                return mm

            def body(now):
                for p in now.steps():
                    kind, s, i = p
                    if kind not in PRODUCTS:
                        continue
                    for q, earlier in dict.fromkeys(now.previous(users[b], p) for b in banks(p)):
                        wait(pe, now, *reader(q), earlier)
                    if kind == "EMB":
                        pe.wait_ge(x_loaded[s], (now.it + 2 - s) * 16)
                        for t in range(2):
                            for c in range(KC):
                                nc.tensor.matmul(ps(p, slice(0, TR), slice(194 * t, 194 * t + D + 1)),
                                                 xb[s][:, c, tile_cols(t)], emb_w[:, c, :],
                                                 start=(c == 0), stop=(c == KC - 1))
                        wait(pe, now, xss_ready, ("X", s, 0))
                        for t in range(2):
                            mm = nc.tensor.matmul(ps(p, slice(0, TR), slice(194 * t + 193, 194 * t + 194)),
                                                  xss[s][:, tile_cols(t)], one_col,
                                                  start=True, stop=True)
                    elif kind == "T1":
                        wait(pe, now, hn_ready, ("LC", s, 0))
                        mm = hidden_transposed(p, hn[s])
                    elif kind == "QK":
                        wait(pe, now, rd_sig["T1"], ("T1", s, 0))
                        for m in range(4):
                            f = 128 * (4 * i + m)
                            at = NT * (m % 2)
                            for n, (c, w, v) in enumerate((c, *wv) for c in range(2) for wv in SPLIT):
                                mm = nc.tensor.matmul(ps(p, slice(0, 128), slice(at, at + NT), m // 2),
                                                      qk_w[:, w, c, f:f + 128], hn_s[s][:, v, c, 0:NT],
                                                      start=(n == 0), stop=(n == 5))
                    elif kind == "PS":
                        wait(pe, now, ss_ready, ("S", s, 0))
                        mm = nc.tensor.matmul(ps(p, slice(0, 128), slice(0, 2 * NT)), pair_sum,
                                              ss[s][:].rearrange("p a t -> p (a t)"), start=True, stop=True)
                    elif kind == "V":
                        for b in range(2):
                            for n, (c, w, v) in enumerate((c, *wv) for c in range(2) for wv in SPLIT):
                                mm = nc.tensor.matmul(ps(p, slice(0, TR), slice(0, INNER // 2), b),
                                                      hn_s[s][:, v, c, tile_cols(i)],
                                                      v_w[:, w, c, INNER // 2 * b:INNER // 2 * (b + 1)],
                                                      start=(n == 0), stop=(n == 5))
                    elif kind in ("SM", "SM2"):
                        if kind == "SM":
                            for n in (1, 3):
                                wait(pe, now, spread[s, n], ("N", s, n), by=96)
                        else:
                            wait(pe, now, rd_sig["QK2"], ("QK2", s, 1))
                            wait(pe, now, ka2_ready, ("QK2", s, 1))
                        for e in range(2):
                            h = 2 * i + e
                            for t in range(2):
                                mm = nc.tensor.matmul(ps(p, slice(0, TR), slice(NT * t, NT * t + NT), e),
                                                      qa[s][:, h if kind == "SM" else h // 4, tile_cols(t)],
                                                      ka[s][:, h, 0:NT], start=True, stop=True)
                    elif kind in ("NT", "NT2"):
                        wait(pe, now, mx_ready if kind == "NT" else mx2_ready, p)
                        mm = transposes(p, lambda t, n: neg[s][0:n, t], 128)
                    elif kind in ("ST", "ST2"):
                        nt = "NT" if kind == "ST" else "NT2"
                        wait(pe, now, rd_sig[nt], (nt, s, 0))
                        for e in range(2):
                            h = 6 * e + i if kind == "ST" else 2 * i + e
                            g = h if kind == "ST" else h // 4
                            for t in range(2):
                                o = ps(p, slice(0, TR), slice(NT * t, NT * t + NT), e)
                                nc.tensor.matmul(o, ka[s][:, h, tile_cols(t)], qa[s][:, g, 0:NT],
                                                 start=True, stop=False)
                                mm = nc.tensor.matmul(o, kb[s][:, h, tile_cols(t)], qb[s][:, g, 0:NT],
                                                      start=False, stop=True)
                    elif kind == "PV":
                        wait(pe, now, rd_sig["ST"], ("ST", s, i))
                        wait(pe, now, rd_sig["V"], ("V", s, 1))
                        eb = ebuf[e_order.index(("ST", s, i)) % EBUFS]
                        for e in range(2):
                            for t in range(2):
                                n = key_rows(t)
                                mm = nc.tensor.matmul(ps(p, slice(0, 128), slice(NT * e, NT * e + NT)),
                                                      vx[s][0:n, t, 2 * i + e, :], eb[0:n, e, t, :],
                                                      start=(t == 0), stop=(t == 1))
                    elif kind == "OP":
                        wait(pe, now, rd_sig["PV"], ("M", s, 5))
                        for t in range(2):
                            for m in range(H // 2):
                                mm = nc.tensor.matmul(ps(p, slice(0, TR), slice(D * t, D * t + D)),
                                                      o_t[s][:, m, tile_cols(t)], out_w[:, m, :],
                                                      start=(m == 0), stop=(m == H // 2 - 1))
                    elif kind == "T2":
                        wait(pe, now, hn2_ready, ("LD", s, 0))
                        mm = hidden_transposed(p, hn[s])
                    elif kind == "G":
                        wait(pe, now, rd_sig["T2"], ("T2", s, 0))
                        for t in range(2):
                            for c in range(2):
                                mm = nc.tensor.matmul(ps(p, slice(0, TR), slice(136 * t, 136 * t + 136)),
                                                      hn2_t[s][:, c, tile_cols(t)], gl_w[:, c, :],
                                                      start=(c == 0), stop=(c == 1))
                    elif kind == "T3":
                        wait(pe, now, hw_ready, ("GB", s, 0))
                        transposes(p, lambda t, n: hw[s][0:n, t], 128)
                        for t in range(2):
                            n = key_rows(t)
                            mm = nc.tensor.transpose(
                                ps(p, slice(0, 3 * (NE + 1)), slice(NT + TO * t, NT + TO * t + n)),
                                comb3[s][0:n, t].rearrange("p a b -> p (a b)"), ident[0:n, 0:n])
                    elif kind == "QK2":
                        wait(pe, now, rd_sig["T3"], ("T3", s, 0))
                        for m in range(G2):
                            o = ps(p, slice(0, 128), slice(NT * (m % 2), NT * (m % 2) + NT), m // 2)
                            f = slice(128 * (G2 * i + m), 128 * (G2 * i + m) + 128)
                            for w, v in SPLIT:
                                for c in range(2):
                                    nc.tensor.matmul(o, qkv2_w[:, w, c, f], hn2_s[s][:, v, c, 0:NT],
                                                     start=(c + w + v == 0), stop=False)
                                nc.tensor.matmul(o, lorab_w[:, w, f], hw_s[s][:, v, 0:NT], start=False, stop=False)
                            mm = nc.tensor.matmul(o, bias2_w[:, f], comb_t[s][:, 0:NT], start=False, stop=True)
                    elif kind == "V2":
                        f = slice(QKV2 - D, QKV2)
                        for t in range(2):
                            o = ps(p, slice(0, TR), slice(D * t, D * t + D))
                            for w, v in SPLIT:
                                for c in range(2):
                                    nc.tensor.matmul(o, hn2_s[s][:, v, c, tile_cols(t)], qkv2_w[:, w, c, f],
                                                     start=(c + w + v == 0), stop=False)
                                nc.tensor.matmul(o, hw_s[s][:, v, tile_cols(t)], lorab_w[:, w, f],
                                                 start=False, stop=False)
                            mm = nc.tensor.matmul(o, comb_t[s][:, tile_cols(t)], bias2_w[:, f],
                                                  start=False, stop=True)
                    elif kind == "PV2":
                        wait(pe, now, rd_sig["ST2"], ("ST2", s, 2 * i + 1))
                        wait(pe, now, rd_sig["V2"], ("V2", s, 0))
                        for t in range(2):
                            n = key_rows(t)
                            for j in range(4):
                                eb = ebuf[e_order.index(("ST2", s, 2 * i + j // 2)) % EBUFS]
                                mm = nc.tensor.matmul(ps(p, slice(32 * j, 32 * j + 32), slice(0, NT)),
                                                      v2[s][0:n, t, 4 * i + j, :], eb[0:n, j % 2, t, :],
                                                      start=(t == 0), stop=(t == 1))
                    elif kind == "OP2":
                        wait(pe, now, o2_ready, ("M2", s, 2))
                        for t in range(2):
                            for m in range(3):
                                mm = nc.tensor.matmul(ps(p, slice(0, TR), slice(D * t, D * t + D)),
                                                      o2_t[s][:, m, tile_cols(t)], proj_w[:, m, :],
                                                      start=(m == 0), stop=(m == 2))
                    mm.then_inc(pe_sig[kind][1], 1)

            passes(pe, body)

        @block.scalar
        def _(act):
            act.wait_ge(consts_loaded, 16 * len(loads))
            act.wait_ge(fills, NFILLS)
            act.wait_ge(setup_dve, 2)
            nc.scalar.preload_act_table_set("natural_log_exp_and_others")
            count = [0]

            def link(ins):
                count[0] += 1
                ins.then_inc(act_chain, 1)
                act.wait_ge(act_chain, count[0])

            def body(now):
                act.sem_clear(act_chain)
                count[0] = 0
                for p in now.steps():
                    kind, s, i = p
                    done = rd_sig[kind][1] if kind in rd_sig else None
                    b = BANK[p]
                    if kind == "X":
                        act.wait_ge(x_loaded[s], (now.it + 2 - s) * 16)
                        wait_free(act, now, sq_users, squares_used)
                        nc.scalar.activation(xsq, xb[s][:], ACT.Square).then_inc(xsq_ready[1], 1)
                    elif kind in ("T1", "T2"):
                        wait(act, now, pe_sig[kind], p)
                        src = psum[0:HC, b, 0:2 * NT].rearrange("p (c t) -> p c t", c=2)
                        dst = hn_s if kind == "T1" else hn2_s
                        if kind == "T2":
                            nc.scalar.copy(hn2_t[s], src)
                        sig = split_T1 if kind == "T1" else split_T2
                        nc.scalar.copy(dst[s][:, 0, :, 0:NT], src).then_inc(sig[1], 1)
                    elif kind == "QK":
                        wait(act, now, pe_sig[kind], p)
                        src = psum[:, b:b + 2, 0:2 * NT]
                        if i == 0:
                            wait_free(act, now, sq_users, squares_used)
                        nc.scalar.activation(
                            qk_sq[:, 4 * i:4 * i + 4, :].rearrange("p (b m) t -> p b (m t)", b=2),
                            src, ACT.Square, scale=1 / WS)
                        nc.scalar.mul(qk[s][:, 4 * i:4 * i + 4, :].rearrange("p (b m) t -> p b (m t)", b=2),
                                      src, 1 / WS).then_inc(done, 1)
                    elif kind == "PS":
                        wait(act, now, pe_sig[kind], p)
                        n2 = nrm[s]
                        nc.scalar.activation(n2, psum[:, b, 0:2 * NT], ACT.Ln, bias=tiny[:]).then_inc(done, 1)
                        wait(act, now, rd_sig[kind], p)
                        link(nc.scalar.activation(n2, n2, ACT.Exp, scale=0.5))
                        link(nc.scalar.activation(n2, n2, ACT.Ln, bias=eps_qk[:]))
                        nc.scalar.activation(n2, n2, ACT.Exp, scale=-0.5).then_inc(rr_ready[1], 1)
                    elif kind == "N" and i % 2 == 1:
                        wait(act, now, qkn_ready, ("N", s, i - 1))
                        q, earlier = now.previous(split_users, p)
                        wait(act, now, spread[q[1:]], q, earlier, by=96)
                        nc.scalar.copy(high[:, :, 0:NT], qk[s][:, 6 * (i // 2):6 * (i // 2) + 6, :]
                                       ).then_inc(high_N[1], 1)
                    elif kind == "V":
                        wait(act, now, pe_sig[kind], p)
                        nc.scalar.mul(
                            vx[s][:, i, :, 0:DH].rearrange("p (b h) d -> p b h d", b=2),
                            psum[0:TR, b:b + 2, 0:INNER // 2].rearrange("p b (h d) -> p b h d", d=DH),
                            1 / WS).then_inc(done, 1)
                    elif kind in ("NT", "NT2"):
                        wait(act, now, pe_sig[kind], p)
                        nc.scalar.copy(qb[s][64:128, 0, 0:NT], psum[64:128, b, 0:NT]).then_inc(neg_copied[1], 1)
                    elif kind in ("ST", "ST2"):
                        wait(act, now, pe_sig[kind], p)
                        n = e_order.index(p)
                        wait_free(act, now, e_users[n % EBUFS], exp_used)
                        nc.scalar.activation(ebuf[n % EBUFS][:].rearrange("p e a t -> p e (a t)"),
                                             psum[0:TR, b:b + 2, 0:2 * NT], ACT.Exp).then_inc(done, 1)
                    elif kind == "PV":
                        wait(act, now, pe_sig[kind], p)
                        n = pv_order.index(p) % 2
                        wait_free(act, now, rinv_users[n], reader)
                        r = rinv[n][:]
                        link(nc.scalar.activation(r, psum[DH:128, b, 0:2 * NT], ACT.Ln))
                        nc.scalar.activation(r, r, ACT.Exp, scale=-1.0).then_inc(rinv_ready[1], 1)
                    elif kind == "PV2":
                        wait(act, now, sums2_ready, p)
                        r = sums2[pv2_order.index(p) % 2][:]
                        link(nc.scalar.activation(r, r, ACT.Ln))
                        nc.scalar.activation(r, r, ACT.Exp, scale=-1.0).then_inc(rinv2_ready[1], 1)
                    elif kind == "G":
                        wait(act, now, gmax_ready, p)
                        nc.scalar.activation(gates[s][:, :, 0:NE], gl[s][:, :, 0:NE], ACT.Exp
                                             ).then_inc(gexp_ready[1], 1)
                    elif kind == "T3":
                        wait(act, now, pe_sig[kind], p)
                        nc.scalar.copy(comb_t[s][:, 0:NT], psum[0:3 * (NE + 1), b, NT:2 * NT])
                        nc.scalar.copy(hw_s[s][:, 0, 0:NT], psum[:, b, 0:NT]).then_inc(split_T3[1], 1)
                    elif kind == "QK2":
                        wait(act, now, pe_sig[kind], p)
                        dst, f = (qa[s], QSCALE / WS) if i == 0 else (high2, 1 / WS)
                        if i == 1:
                            wait_free(act, now, high2_users, reader)
                        nc.scalar.mul(dst[:, 0:2, 0:NT],
                                      psum[:, b, 0:2 * NT].rearrange("p (m t) -> p m t", m=2), f)
                        nc.scalar.mul(dst[:, 2, 0:NT], psum[:, b + 1, 0:NT], f).then_inc(high_QK2[1], 1)
                        if i == 1:
                            wait(act, now, high_QK2, p)
                            for j in range(4):
                                a = nc.scalar.mul(ka[s][:].rearrange("p (g j) t -> p g j t", j=4)[:, :, j, :],
                                                  high2[:], masks[:, j:j + 1])
                            a.then_inc(ka2_ready[1], 1)
                    elif kind == "V2":
                        wait(act, now, pe_sig[kind], p)
                        nc.scalar.mul(v2[s][:, :, :, 0:DH2],
                                      psum[0:TR, b, 0:2 * D].rearrange("p (a h d) -> p a h d", a=2, d=DH2),
                                      1 / WS).then_inc(done, 1)

            passes(act, body)

        @block.vector
        def _(dve):
            count = [0]

            def link(ins):
                count[0] += 1
                ins.then_inc(dve_chain, 1)
                dve.wait_ge(dve_chain, count[0])

            dve.wait_ge(consts_loaded, 16 * len(loads))
            dve.wait_ge(fills, NFILLS)
            nc.vector.tensor_tensor(emb_w[:, :, 0:D], emb_raw,
                                    ln1_sb[:].unsqueeze(2).broadcast_to([128, KC, D]), ALU.mult
                                    ).then_inc(setup_dve, 1)
            nc.vector.reciprocal(inv_scale[:], scale_sb[:])
            for s in range(2):
                nc.vector.tensor_copy(kb[s][64:128], sel_raw[64:128].broadcast_to([64, H, NTP]))

            def split_weights(dst, raw):
                nc.vector.tensor_scalar(dst(0), raw, WS, None, ALU.mult).then_inc(setup_w, 1)
                splits[0] += 1
                dve.wait_ge(setup_w, splits[0])
                nc.vector.scalar_tensor_tensor(out=dst(1), in0=raw, scalar=WS, in1=dst(0),
                                               op0=ALU.mult, op1=ALU.subtract)

            splits = [0]
            split_weights(lambda v: qk_w[:, v], qk_raw)
            split_weights(lambda v: v_w[:, v], v_raw)
            split_weights(lambda v: qkv2_w[:, v], qkv2_raw)
            split_weights(lambda v: lorab_w[:, v], lorab_raw[:, 0])
            nc.vector.tensor_scalar(bias2_raw[:, 0], bias2_raw[:, 0], WS, None, ALU.mult).then_inc(setup_w, 1)
            dve.wait_ge(setup_w, 5)
            nc.vector.tensor_copy(bias2_w[:], bias2_raw[:, 0]).then_inc(setup_w, 1)
            dve.wait_ge(setup_w, 6)
            nc.vector.scalar_tensor_tensor(out=bias2_w[:], in0=bias2_w[:], scalar=low_row, in1=bias2_raw[:, 0],
                                           op0=ALU.mult, op1=ALU.add)
            dve.wait_ge(setup_pe, 1)
            nc.vector.tensor_copy(emb_cs[:], psum[0:TR, 0, 0:D])
            nc.vector.tensor_tensor(emb_b[:], tok_b[:, 0, :], psum[0:TR, 1, 0:D], ALU.add
                                    ).then_inc(setup_dve, 1)
            dve.wait_ge(setup_dve, 2)

            def variance(s, src):
                for t in range(2):
                    a = nc.vector.bn_stats(st6[s][:, t, :], src[:, t, :])
                link(a)
                for t in range(2):
                    a = nc.vector.bn_aggr(mv[s][:, t, :], st6[s][:, t, :])
                a.then_inc(var_ready[1], 1)

            def normalise(s, src, dst):
                for t in range(2):
                    a = nc.vector.tensor_scalar(dst[:, t, :], src[:, t, :], mv[s][:, t, 0:1],
                                                rstd[s][:, t:t + 1], ALU.subtract, ALU.mult)
                return a

            def body(now):
                dve.sem_clear(dve_chain)
                count[0] = 0
                for p in now.steps():
                    kind, s, i = p
                    done = rd_sig[kind][1] if kind in rd_sig else None
                    b = BANK[p]
                    if kind == "X":
                        wait(dve, now, xsq_ready, p)
                        nc.vector.tensor_reduce(xss[s][:], xsq.rearrange("p c t -> p t c"), AX.X, ALU.add
                                                ).then_inc(xss_ready[1], 1)
                    elif kind == "EMB":
                        wait(dve, now, pe_sig[kind], p)
                        sums = psum[0:TR, b, 0:388].rearrange("p (t f) -> p t f", t=2)
                        link(nc.vector.tensor_scalar(nmean[s][:], sums[:, :, D], -1.0 / PD, None, ALU.mult))
                        link(nc.vector.tensor_tensor(msq[:], nmean[s][:], nmean[s][:], ALU.mult))
                        nc.vector.scalar_tensor_tensor(out=mv[s][:, :, 1], in0=sums[:, :, D + 1],
                                                       scalar=1.0 / PD, in1=msq[:], op0=ALU.mult,
                                                       op1=ALU.subtract).then_inc(var_ready[1], 1)
                        for t in range(2):
                            a = nc.vector.scalar_tensor_tensor(out=lnt[s][:, t, :], in0=emb_cs[:],
                                                               scalar=nmean[s][:, t:t + 1],
                                                               in1=sums[:, t, 0:D],
                                                               op0=ALU.mult, op1=ALU.add)
                        a.then_inc(done, 1)
                    elif kind == "LA":
                        wait(dve, now, rd_sig["EMB"], ("EMB", s, 0))
                        wait(dve, now, rstd_ready, ("EMB", s, 0))
                        for t in range(2):
                            a = nc.vector.scalar_tensor_tensor(out=lnt[s][:, t, :], in0=lnt[s][:, t, :],
                                                               scalar=rstd[s][:, t:t + 1], in1=emb_b[:],
                                                               op0=ALU.mult, op1=ALU.add)
                        link(a)
                        variance(s, lnt[s])
                    elif kind == "LB":
                        wait(dve, now, rstd_ready, ("LA", s, 0))
                        link(normalise(s, lnt[s], h0[s]))
                        link(nc.vector.tensor_tensor(h0[s][:], h0[s][:], tokc[:, 0], ALU.mult))
                        link(nc.vector.tensor_tensor(h0[s][:], h0[s][:], tokc[:, 1], ALU.add))
                        variance(s, h0[s])
                    elif kind == "LC":
                        wait(dve, now, rstd_ready, ("LB", s, 0))
                        normalise(s, h0[s], hn[s]).then_inc(hn_ready[1], 1)
                    elif kind in ("T1", "T2"):
                        wait(dve, now, split_T1 if kind == "T1" else split_T2, p)
                        dst = (hn_s if kind == "T1" else hn2_s)[s]
                        nc.vector.tensor_tensor(dst[:, 1, :, 0:NT],
                                                psum[0:HC, b, 0:2 * NT].rearrange("p (c t) -> p c t", c=2),
                                                dst[:, 0, :, 0:NT], ALU.subtract).then_inc(done, 1)
                    elif kind == "S":
                        wait(dve, now, rd_sig["QK"], ("QK", s, 2))
                        for a in range(2):
                            r = nc.vector.tensor_reduce(ss[s][:, a, :],
                                                        qk_sq[:, 6 * a:6 * a + 6, :].rearrange("p m t -> p t m"),
                                                        AX.X, ALU.add)
                        r.then_inc(ss_ready[1], 1)
                    elif kind == "N":
                        if i == 0:
                            wait(dve, now, rr_ready, ("PS", s, 0))
                            for m in range(6):
                                a = nc.vector.scalar_tensor_tensor(out=qk[s][:, m, :], in0=qk[s][:, m, :],
                                                                   scalar=inv_scale[:, m:m + 1],
                                                                   in1=nrm[s][:, 0:NT],
                                                                   op0=ALU.mult, op1=ALU.mult)
                        elif i == 2:
                            a = nc.vector.tensor_tensor(qk[s][:, 6:12, :], qk[s][:, 6:12, :],
                                                        nrm[s][:, NT:2 * NT].unsqueeze(1).broadcast_to([128, 6, NT]),
                                                        ALU.mult)
                        else:
                            wait(dve, now, high_N, p)
                            a = nc.vector.tensor_tensor(low[:, :, 0:NT], qk[s][:, 6 * (i // 2):6 * (i // 2) + 6, :],
                                                        high[:, :, 0:NT], ALU.subtract)
                        a.then_inc(qkn_ready[1], 1)
                    elif kind in ("SM", "SM2"):
                        wait(dve, now, pe_sig[kind], p)
                        nc.vector.tensor_reduce(
                            mx[s][:, :, 2 * i:2 * i + 2].rearrange("p a e -> p e a"),
                            psum[0:TR, b:b + 2, 0:2 * NT].rearrange("p e (a t) -> p e a t", a=2),
                            AX.X, ALU.max).then_inc(done, 1)
                        if i == 5:
                            wait(dve, now, rd_sig[kind], p)
                            ready = mx_ready if kind == "SM" else mx2_ready
                            nc.vector.tensor_scalar(neg[s][:, :, 64:64 + H], mx[s][:], -1.0, None, ALU.mult
                                                    ).then_inc(ready[1], 1)
                    elif kind in ("NT", "NT2"):
                        wait(dve, now, neg_copied, p)
                        n = (H if kind == "NT" else G2) - 1
                        nc.vector.tensor_copy(qb[s][64:128, 1:1 + n, :],
                                              qb[s][64:128, 0:1, :].broadcast_to([64, n, NTP])).then_inc(done, 1)
                    elif kind == "M":
                        done, q = rd_sig["PV"][1], ("PV", s, i)
                        b = BANK[q]
                        wait(dve, now, rinv_ready, q)
                        r = rinv[pv_order.index(q) % 2]
                        for e in range(2):
                            a = nc.vector.tensor_tensor(o_t[s][DH * e:DH * e + DH, i, :],
                                                        psum[0:DH, b, NT * e:NT * e + NT],
                                                        r[:, NT * e:NT * e + NT], ALU.mult)
                        a.then_inc(done, 1)
                    elif kind == "OP":
                        dve.wait_ge(stored[s], now.it * 48)
                        wait(dve, now, h0_ready, ("LC", s, 0))
                        wait(dve, now, pe_sig[kind], p)
                        nc.vector.tensor_tensor(h1[s][:].rearrange("p a d -> p (a d)"), psum[0:TR, b, 0:2 * D],
                                                h0[s][:].rearrange("p a d -> p (a d)"), ALU.add).then_inc(done, 1)
                        wait(dve, now, rd_sig[kind], p)
                        variance(s, h1[s])
                    elif kind == "LD":
                        wait(dve, now, rstd_ready, ("OP", s, 0))
                        normalise(s, h1[s], hn[s]).then_inc(hn2_ready[1], 1)
                    elif kind == "G":
                        wait(dve, now, pe_sig[kind], p)
                        nc.vector.tensor_tensor(gl[s][:], psum[0:TR, b, 0:272].rearrange("p (t f) -> p t f", t=2),
                                                b_gl.unsqueeze(1).broadcast_to([TR, 2, 136]), ALU.add
                                                ).then_inc(done, 1)
                        wait(dve, now, rd_sig[kind], p)
                        link(nc.vector.tensor_reduce(gmax[:], gl[s][:, :, 0:NE], AX.X, ALU.max))
                        nc.vector.tensor_tensor(gl[s][:, :, 0:NE], gl[s][:, :, 0:NE],
                                                gmax[:].unsqueeze(2).broadcast_to([TR, 2, NE]), ALU.subtract
                                                ).then_inc(gmax_ready[1], 1)
                    elif kind == "GB":
                        wait(dve, now, gexp_ready, ("G", s, 0))
                        link(nc.vector.tensor_reduce(gsum[:], gates[s][:, :, 0:NE], AX.X, ALU.add))
                        link(nc.vector.reciprocal(gsum[:], gsum[:]))
                        link(nc.vector.tensor_scalar(gsum[:], gsum[:], LORA_SCALE, None, ALU.mult))
                        for t in range(2):
                            a = nc.vector.max(top8[:, t, :], gates[s][:, t, :])
                        link(a)
                        link(nc.vector.memset(top8[:, :, 2:8], -1.0))
                        for t in range(2):
                            a = nc.vector.match_replace(rest[:, t, :], top8[:, t, :], gates[s][:, t, :], 0.0)
                        link(a)
                        link(nc.vector.tensor_tensor(rest[:, :, 0:NE], gates[s][:, :, 0:NE], rest[:, :, 0:NE],
                                                     ALU.subtract))
                        link(nc.vector.tensor_tensor(comb[s][:, :, 0:NE], rest[:, :, 0:NE],
                                                     gsum[:].unsqueeze(2).broadcast_to([TR, 2, NE]), ALU.mult))
                        nc.vector.tensor_copy(comb_h[:], comb[s][:])
                        for t in range(2):
                            a = nc.vector.tensor_tensor(
                                hw[s][:, t].rearrange("p (e r) -> p e r", e=NE),
                                hw[s][:, t].rearrange("p (e r) -> p e r", e=NE),
                                comb[s][:, t, 0:NE].unsqueeze(2).broadcast_to([TR, NE, RANK]), ALU.mult)
                        link(a)
                        for part in (0, 2):
                            nc.vector.tensor_copy(comb3[s][:, :, part, :], comb_h[:])
                        nc.vector.tensor_tensor(comb3[s][:, :, 1, :], comb[s][:], comb_h[:], ALU.subtract
                                                ).then_inc(hw_ready[1], 1)
                    elif kind == "T3":
                        wait(dve, now, split_T3, p)
                        nc.vector.tensor_tensor(hw_s[s][:, 1, 0:NT], psum[:, b, 0:NT], hw_s[s][:, 0, 0:NT],
                                                ALU.subtract).then_inc(done, 1)
                    elif kind == "QK2":
                        wait(dve, now, high_QK2, p)
                        pair = psum[:, b, 0:2 * NT].rearrange("p (m t) -> p m t", m=2)
                        if i == 0:
                            nc.vector.tensor_copy(qb[s][0:64, 0:G2, :], qa[s][0:64, 0:G2, :])
                            for dst, src in ((qa[s][64:128, 0:2, 0:NT], pair[64:128]),
                                             (qa[s][64:128, 2, 0:NT], psum[64:128, b + 1, 0:NT])):
                                a = nc.vector.scalar_tensor_tensor(out=dst, in0=src, scalar=QSCALE / WS, in1=dst,
                                                                   op0=ALU.mult, op1=ALU.subtract)
                        else:
                            for j, src in ((slice(0, 2), pair[0:64]), (2, psum[0:64, b + 1, 0:NT])):
                                a = nc.vector.scalar_tensor_tensor(out=low2[:, j, 0:NT], in0=src, scalar=1 / WS,
                                                                   in1=high2[0:64, j, 0:NT],
                                                                   op0=ALU.mult, op1=ALU.subtract)
                            link(a)
                            for j in range(4):
                                a = nc.vector.tensor_scalar(
                                    kb[s][0:64].rearrange("p (g j) t -> p g j t", j=4)[:, :, j, :], low2[:],
                                    masks[0:64, j:j + 1], None, ALU.mult)
                        a.then_inc(done, 1)
                    elif kind == "PV2":
                        wait(dve, now, pe_sig[kind], p)
                        o = o2_t[s][:, i, :]
                        link(nc.vector.tensor_copy(o, psum[:, b, 0:NT]))
                        r = sums2[pv2_order.index(p) % 2]
                        nc.vector.stream_shuffle(r[:], o, [j + 16 if j < 16 else j for j in range(32)]
                                                 ).then_inc(done, 1)
                    elif kind == "M2":
                        wait(dve, now, rinv2_ready, ("PV2", s, i))
                        r = sums2[pv2_order.index(("PV2", s, i)) % 2]
                        o = o2_t[s][:, i, :]
                        nc.vector.tensor_tensor(o, o, r[:], ALU.mult).then_inc(o2_ready[1], 1)
                    elif kind == "OP2":
                        wait(dve, now, h1_ready, ("LD", s, 0))
                        wait(dve, now, pe_sig[kind], p)
                        nc.vector.tensor_tensor(res[s][:].rearrange("p a d -> p (a d)"), psum[0:TR, b, 0:2 * D],
                                                h1[s][:].rearrange("p a d -> p (a d)"), ALU.add
                                                ).then_inc(done, 1)

            passes(dve, body)


def kernel(x, L0_tok_ln1_g, L0_tok_ln1_b, L0_tok_W, L0_tok_b, L0_tok_ln2_g, L0_tok_ln2_b, L0_tok_cls,
           L0_attn_w_qkv, L0_attn_w_out, L0_attn_b_out, L0_attn_scale, L0_ffn_Wg, L0_ffn_bg, L0_ffn_Wqkv,
           L0_ffn_bqkv, L0_ffn_Wproj, L0_ffn_bproj, L0_ffn_A, L0_ffn_ba, L0_ffn_Bm, L0_ffn_bb):
    import concourse.bacc as bacc
    from concourse.bass_utils import run_bass_kernel_spmd

    f = np.float32
    p = np.asarray(x).reshape(B, 3, 14, 16, 14, 16).transpose(0, 3, 5, 1, 2, 4).reshape(B, KC, 128, NP)
    x_t = np.zeros((B, 128, KC, NT), f)
    x_t[..., :NP] = p.transpose(0, 2, 1, 3)

    def chunks(a, rows):
        a = np.asarray(a)
        return a.reshape(-1, rows, a.shape[-1]).transpose(1, 0, 2)

    ln1 = chunks(np.asarray(L0_tok_ln1_g).reshape(PD, 1), 128)[:, :, 0]
    ln1_bias = np.repeat(chunks(np.asarray(L0_tok_ln1_b).reshape(PD, 1), 128), TR, axis=2)
    tok_const = np.zeros((TR, 2, 2, D), f)
    tok_const[:, 0], tok_const[:, 1] = L0_tok_ln2_g, L0_tok_ln2_b
    tok_const[TR - 1, 0, 1] = 0
    tok_const[TR - 1, 1, 1] = np.asarray(L0_tok_cls)[0, 0]
    w_t = np.asarray(L0_attn_w_qkv).T
    w2 = np.asarray(L0_ffn_Wqkv).T
    twice = np.repeat(np.arange(2 * D).reshape(2 * G2, 1, 64), 2, axis=1).reshape(-1)
    order = np.r_[twice, 2 * D:3 * D]
    w_gl = np.concatenate([np.asarray(L0_ffn_Wg), np.asarray(L0_ffn_A).reshape(NE * RANK, D)]).T
    w_lora_b = np.asarray(L0_ffn_Bm).transpose(0, 2, 1).reshape(NE * RANK, 1, 3 * D)[:, :, order]
    w_bias2 = np.concatenate([np.asarray(L0_ffn_bb), np.asarray(L0_ffn_bqkv)[None]])[:, None, order]
    w_bias2 = np.concatenate([w_bias2] * 3)
    w_proj = np.zeros((3, 4, 32, D), f)
    w_proj[:, :, :DH2] = np.asarray(L0_ffn_Wproj).T.reshape(3, 4, DH2, D)
    scale = np.repeat(np.asarray(L0_attn_scale).reshape(H // 2, 2), DH, axis=1).T
    row = np.concatenate([np.asarray(L0_attn_b_out), np.asarray(L0_ffn_bproj), np.asarray(L0_ffn_bg),
                          np.asarray(L0_ffn_ba).reshape(-1)])
    row_const = np.repeat(row[None], TR, axis=0)
    mats = np.zeros((128, 261), f)
    r = np.arange(128)
    mats[r, r] = 1
    mats[:, 128:256] = (r[:, None] % DH == r[None, :] % DH)
    mats[r, 256 + r % 64 // DH2] = 1
    mats[2 * (NE + 1):3 * (NE + 1), 260] = -1
    sel = np.zeros((128, H, 1), f)
    sel[64 + np.arange(H), np.arange(H)] = 1

    arrays = {
        "x_t": x_t, "w_emb": chunks(L0_tok_W, 128), "ln1": ln1, "ln1_bias": ln1_bias, "tok_const": tok_const,
        "tok_bias": np.repeat(np.asarray(L0_tok_b)[None, None], TR, axis=0),
        "w_qk": chunks(w_t[:, :2 * INNER], HC), "w_v": chunks(w_t[:, 2 * INNER:], HC),
        "w_out": chunks(np.asarray(L0_attn_w_out).T, 128), "w_gl": chunks(w_gl, HC),
        "w_qkv2": chunks(w2[:, order], HC), "w_lora_b": w_lora_b, "w_bias2": w_bias2,
        "w_proj": chunks(w_proj.reshape(384, D), 128), "scale": scale, "row_const": row_const,
        "mats": mats, "sel": sel,
    }
    arrays = {k: np.ascontiguousarray(v) for k, v in arrays.items()}
    nc = bacc.Bacc("TRN2", target_bir_lowering=False, num_devices=1)
    args = [nc.dram_tensor(k, v.shape, mybir.dt.from_np(v.dtype), kind="ExternalInput").ap()
            for k, v in arrays.items()]
    out = nc.dram_tensor("out", (B, NT, D), mybir.dt.float32, kind="ExternalOutput").ap()
    vit_tower(nc, *args, out)
    return run_bass_kernel_spmd(nc, [arrays], core_ids=[0]).results[0]["out"]
```
